# Optimizing a Trainium2 kernel written in Bass

```python
import numpy as np
import jax
import jax.numpy as jnp

def _softmax(x, axis=-1):
    return jax.nn.softmax(x, axis=axis)

def _gelu(x):
    return jax.nn.gelu(x, approximate=True)

def _silu(x):
    return jax.nn.silu(x)

def _sigmoid(x):
    return jax.nn.sigmoid(x)

def _layernorm(x, axis=-1, eps=1e-05):
    m = jnp.mean(x, axis=axis, keepdims=True)
    v = jnp.var(x, axis=axis, keepdims=True)
    return (x - m) / jnp.sqrt(v + eps)

def _scatter_add(tgt, idx, src, axis=0):
    return tgt.at[idx].add(src)

def _segment_sum(src, seg, n):
    return jax.ops.segment_sum(src, seg, n)
kernel_name = 'mk_cond_resid_d2_seqx_r8_9a8d7d'

def setup_inputs(seed: int=0):
    np.random.seed(seed)
    _w = jnp.asarray

    def _rec_inputs():
        import jax
        import jax.numpy as jnp
        _rk = jax.random.key(seed)
        x = -0.003407 + 1.001 * jax.random.normal(jax.random.fold_in(_rk, 1), (128, 32, 256), jnp.float32)
        _lenS = 32 - jax.random.randint(jax.random.fold_in(_rk, 7), (128,), 0, max(1, 32 // 4) + 1, jnp.int32)
        _lenS2 = 32 - jax.random.randint(jax.random.fold_in(_rk, 8), (128,), 0, max(1, 32 // 4) + 1, jnp.int32)
        itok_Bx257_0_4111 = jax.random.randint(jax.random.fold_in(_rk, 11), (128, 257), 0, 514, jnp.int32)
        itok_B_37_3939 = jax.random.randint(jax.random.fold_in(_rk, 12), (128,), 37, 3940, jnp.int32)
        itok_B_0_7 = jax.random.randint(jax.random.fold_in(_rk, 13), (128,), 0, 8, jnp.int32)
        fside_8xS_0 = -0.00162727 + 0.0609077 * jax.random.normal(jax.random.fold_in(_rk, 14), (8, 32), jnp.float32)
        return (x, itok_Bx257_0_4111, itok_B_37_3939, itok_B_0_7, fside_8xS_0)
    x, itok_Bx257_0_4111, itok_B_37_3939, itok_B_0_7, fside_8xS_0 = _rec_inputs()

    def _L0_cond_setup():
        import jax, jax.numpy as jnp
        import numpy as np
        H, G, HD = (8, 4, 32)
        GSZ = H // G
        BLOCK = 16
        WINDOW = 128
        SCALE = 256.0 ** (-0.5)
        EPS = 1e-06
        THETA = 10000.0
        B, T, D = (16, 4, 256)
        NBLK = 257

        def _rms(x, scale):
            var = jnp.mean(x * x, axis=-1, keepdims=True)
            return x * jax.lax.rsqrt(var + EPS) * (1.0 + scale)

        def _rope(x, pos):
            half = HD // 2
            inv = 1.0 / THETA ** (jnp.arange(half, dtype=jnp.float32) / half)
            ang = pos[:, :, None].astype(jnp.float32) * inv
            cos = jnp.cos(ang)[:, None, :, :]
            sin = jnp.sin(ang)[:, None, :, :]
            x1, x2 = (x[..., :half], x[..., half:])
            return jnp.concatenate([x1 * cos - x2 * sin, x2 * cos + x1 * sin], axis=-1)
        key = jax.random.key(seed)
        ks = jax.random.split(key, 10)
        inv_d = 1.0 / np.sqrt(D)
        return {'x': jax.random.normal(ks[0], (B, T, D), jnp.float32), 'Wq': jax.random.normal(ks[1], (H * HD, D), jnp.float32) * inv_d, 'Wk': jax.random.normal(ks[2], (G * HD, D), jnp.float32) * inv_d, 'Wv': jax.random.normal(ks[3], (G * HD, D), jnp.float32) * inv_d, 'Wo': jax.random.normal(ks[4], (D, H * HD), jnp.float32) * inv_d, 'q_norm_scale': jax.random.normal(ks[5], (HD,), jnp.float32) * 0.02, 'k_norm_scale': jax.random.normal(ks[6], (HD,), jnp.float32) * 0.02, 'k_blocks': jax.random.normal(ks[7], (B * NBLK, G, BLOCK, HD), jnp.float32), 'v_blocks': jax.random.normal(ks[8], (B * NBLK, G, BLOCK, HD), jnp.float32), 'block_tables': jnp.arange(B * NBLK, dtype=jnp.int32).reshape(B, NBLK), 'kv_lens': jax.random.randint(ks[9], (B,), 0, 512, dtype=jnp.int32)}
    _L0_cond_all = _L0_cond_setup()
    _L0_cond_in = {k: v for k, v in _L0_cond_all.items() if k in ('Wq', 'Wk', 'Wv', 'Wo', 'q_norm_scale', 'k_norm_scale', 'k_blocks', 'v_blocks')}
    del _L0_cond_all

    def _L1_cond_setup():
        import jax, jax.numpy as jnp
        import numpy as np
        B, C, T = (64, 32, 256)
        D, N = (32, 8)
        key = jax.random.key(seed)
        k_x, k_s, k_w, k_b = jax.random.split(key, 4)
        scale = 1.0 / np.sqrt(C)
        x = jax.random.normal(k_x, (B, C, T), dtype=jnp.float32)
        subjects = jax.random.randint(k_s, (B,), 0, N, dtype=jnp.int64)
        weights = jax.random.normal(k_w, (N, C, D), dtype=jnp.float32) * scale
        bias = jax.random.normal(k_b, (N, D), dtype=jnp.float32) * scale
        return {'x': x, 'subjects': subjects, 'weights': weights, 'bias': bias}
    _L1_cond_all = _L1_cond_setup()
    _L1_cond_in = {k: v for k, v in _L1_cond_all.items() if k in ('weights',)}
    del _L1_cond_all
    return {'x': x, 'itok_Bx257_0_4111': itok_Bx257_0_4111, 'itok_B_37_3939': itok_B_37_3939, 'itok_B_0_7': itok_B_0_7, 'fside_8xS_0': fside_8xS_0, 'L0_cond_Wq': _L0_cond_in['Wq'], 'L0_cond_Wk': _L0_cond_in['Wk'], 'L0_cond_Wv': _L0_cond_in['Wv'], 'L0_cond_Wo': _L0_cond_in['Wo'], 'L0_cond_q_norm_scale': _L0_cond_in['q_norm_scale'], 'L0_cond_k_norm_scale': _L0_cond_in['k_norm_scale'], 'L0_cond_k_blocks': _L0_cond_in['k_blocks'], 'L0_cond_v_blocks': _L0_cond_in['v_blocks'], 'L1_cond_weights': _L1_cond_in['weights']}

def reference(x, itok_Bx257_0_4111, itok_B_37_3939, itok_B_0_7, fside_8xS_0, L0_cond_Wq, L0_cond_Wk, L0_cond_Wv, L0_cond_Wo, L0_cond_q_norm_scale, L0_cond_k_norm_scale, L0_cond_k_blocks, L0_cond_v_blocks, L1_cond_weights):
    import jax
    import jax.numpy as jnp

    def _L0_cond_ref(x, Wq, Wk, Wv, Wo, q_norm_scale, k_norm_scale, k_blocks, v_blocks, block_tables, kv_lens):
        import jax, jax.numpy as jnp
        import numpy as np
        H, G, HD = (8, 4, 32)
        GSZ = H // G
        BLOCK = 16
        WINDOW = 128
        SCALE = 256.0 ** (-0.5)
        EPS = 1e-06
        THETA = 10000.0
        B, T, D = (16, 4, 256)
        NBLK = 257

        def _rms(x, scale):
            var = jnp.mean(x * x, axis=-1, keepdims=True)
            return x * jax.lax.rsqrt(var + EPS) * (1.0 + scale)

        def _rope(x, pos):
            half = HD // 2
            inv = 1.0 / THETA ** (jnp.arange(half, dtype=jnp.float32) / half)
            ang = pos[:, :, None].astype(jnp.float32) * inv
            cos = jnp.cos(ang)[:, None, :, :]
            sin = jnp.sin(ang)[:, None, :, :]
            x1, x2 = (x[..., :half], x[..., half:])
            return jnp.concatenate([x1 * cos - x2 * sin, x2 * cos + x1 * sin], axis=-1)
        Bx, Tx, _ = x.shape
        q = jnp.einsum('btd,od->bto', x, Wq).reshape(Bx, Tx, H, HD).transpose(0, 2, 1, 3)
        k = jnp.einsum('btd,od->bto', x, Wk).reshape(Bx, Tx, G, HD).transpose(0, 2, 1, 3)
        v = jnp.einsum('btd,od->bto', x, Wv).reshape(Bx, Tx, G, HD).transpose(0, 2, 1, 3)
        q = _rms(q, q_norm_scale)
        k = _rms(k, k_norm_scale)
        pos = kv_lens[:, None] + jnp.arange(Tx, dtype=jnp.int32)
        q = _rope(q, pos)
        k = _rope(k, pos)
        slot = pos // BLOCK
        off = pos % BLOCK
        blk = jnp.take_along_axis(block_tables, slot, axis=1)
        k_blocks = k_blocks.at[blk, :, off, :].set(k.transpose(0, 2, 1, 3))
        v_blocks = v_blocks.at[blk, :, off, :].set(v.transpose(0, 2, 1, 3))
        k_all = k_blocks[block_tables].transpose(0, 2, 1, 3, 4).reshape(Bx, G, -1, HD)
        v_all = v_blocks[block_tables].transpose(0, 2, 1, 3, 4).reshape(Bx, G, -1, HD)
        S = k_all.shape[2]
        qg = q.reshape(Bx, G, GSZ, Tx, HD)
        scores = jnp.einsum('bghtd,bgsd->bghts', qg, k_all) * SCALE
        kpos = jnp.arange(S, dtype=jnp.int32)
        allowed = (kpos[None, None, :] <= pos[:, :, None]) & (kpos[None, None, :] > pos[:, :, None] - WINDOW)
        scores = jnp.where(allowed[:, None, None, :, :], scores, -jnp.inf)
        p = jax.nn.softmax(scores, axis=-1)
        o = jnp.einsum('bghts,bgsd->bghtd', p, v_all).reshape(Bx, H, Tx, HD)
        o = o.transpose(0, 2, 1, 3).reshape(Bx, Tx, H * HD)
        return jnp.einsum('bto,do->btd', o, Wo)

    def _L1_cond_ref(x, subjects, weights, bias):
        import jax, jax.numpy as jnp
        import numpy as np
        B, C, T = (64, 32, 256)
        D, N = (32, 8)
        w = weights[subjects]
        b = bias[subjects]
        out = jnp.einsum('bct,bcd->bdt', x, w)
        out = out + b[:, :, None]
        return out
    x = x + _L0_cond_ref(x, L0_cond_Wq, L0_cond_Wk, L0_cond_Wv, L0_cond_Wo, L0_cond_q_norm_scale, L0_cond_k_norm_scale, L0_cond_k_blocks, L0_cond_v_blocks, itok_Bx257_0_4111, itok_B_37_3939)
    x = x + _L1_cond_ref(x, itok_B_0_7, L1_cond_weights, fside_8xS_0)
    return x

_drawn_inputs = setup_inputs


def setup_inputs(seed=0):
    import zlib

    import numpy as np

    out = dict(_drawn_inputs(seed))
    spreads = {}
    factors = {'L0_cond_q_norm_scale': 64.0, 'L0_cond_k_norm_scale': 64.0}
    for name, (base, spread) in spreads.items():
        noise = np.random.default_rng([zlib.crc32(name.encode()), seed]).standard_normal(out[name].shape)
        drawn = base * np.exp(spread * noise) if base else spread * noise
        out[name] = jnp.asarray(drawn.astype(out[name].dtype))
    for name, factor in factors.items():
        out[name] = (out[name] * factor).astype(out[name].dtype)
    return out
```

```python
from contextlib import ExitStack

import concourse.bass as bass
from concourse import mybir

ALU = mybir.AluOpType
ACT = mybir.ActivationFunctionType
AX = mybir.AxisListType.X
F32 = mybir.dt.float32
BF16 = mybir.dt.bfloat16
I32 = mybir.dt.int32
I16 = mybir.dt.int16

P = 128
B, T, D = 128, 32, 256
G, M, HD = 4, 2, 32
HALF = HD // 2
GH = G * HD
BLOCK = 16
NBLK = 257
CBLK = 16 * NBLK
WINDOW = 128
TILES = B * T // P
BT = P // T
ROW = 2 * GH
PAIR = 2
NR = 80
WIN = PAIR * NR
NSUB = 8
NW = 3
JW = WINDOW // BLOCK + 3
RB = BLOCK // PAIR
RING = 8
GT = 4
NGRP = TILES // GT
SCALE = float(D) ** -0.5
EPS = 1e-6
BIG = 1.0e30
MISS = 131072.0
MAGIC = 12582912.0
INV2PI = 0.15915494309189535
TWO_PI = (6.28125, 0.00193500518798828125, 3.019915981956753e-07)
HALF_PI = 1.5707963267948966
PI_IN = 3.1415925

CONST_COLS = [("iota", NBLK), ("upos", WIN), ("inv", HALF), ("jwin", JW), ("tcol", 1), ("own", 2),
              ("oprow", RB), ("eps", 1), ("ident", P), ("dmask", T), ("blk1", P), ("bdm", BT), ("idxrow", NW * B)]
CO = {}
NCONST = 0
for _name, _w in CONST_COLS:
    CO[_name] = (NCONST, NCONST + _w)
    NCONST += _w


def attention_kernel(nc, xT, x, table, p0, p0T, subjT, wkvT, wqT, woT, qs, ks, cache, wsub, consts, sel4, out):
    key_dram = nc.dram_tensor("key_scratch", [B, 2 * BLOCK], I16, kind="Internal").ap()
    dst_dram = nc.dram_tensor("dst_scratch", [B, T], F32, kind="Internal").ap()
    ent_dram = nc.dram_tensor("entry_scratch", [B, NW], F32, kind="Internal").ap()
    merged = nc.dram_tensor("merged_blocks", [B * NW * BLOCK, ROW], F32, kind="Internal").ap()
    mask_dram = nc.dram_tensor("mask_scratch", [TILES, T, BT, WIN], BF16, kind="Internal").ap()

    with ExitStack() as ctx:
        def sb(name, shape, dt=F32):
            return ctx.enter_context(nc.sbuf_tensor(name, shape, dt))

        def sem(name):
            return ctx.enter_context(nc.semaphore(name))

        bank = [ctx.enter_context(nc.psum_tensor(f"bank{i}", [P, 512], F32)) for i in range(8)]

        cst = sb("cst", [P, NCONST])
        sel4_sb = sb("sel4_sb", [BT, P])
        wkv = sb("wkv", [P, 2, 2 * GH])
        wq = sb("wq", [P, 2, 2 * GH])
        wo = sb("wo", [P, M, D])
        qs_sb = sb("qs_sb", [P, HD])
        ks_sb = sb("ks_sb", [P, HD])
        tab_i = sb("tab_i", [P, NBLK], I32)
        tab = sb("tab", [P, NBLK])
        p0_i = sb("p0_i", [P, 3], I32)
        pra = sb("pra", [P, 3])
        slot = sb("slot", [P, JW])
        blkw = sb("blkw", [P, JW])
        junk = sb("junk", [P, NBLK])
        ents = sb("ents", [P, B * NW])
        repb = sb("repb", [P, JW])
        hit = sb("hit", [P, 2, JW])
        blk_i = sb("blk_i", [P, NW], I32)
        rows88 = sb("rows88", [P, 2, JW * RB])
        sel9 = sb("sel9", [P, RB + 1])
        rows = sb("rows", [P, 2, NR])
        gidx = sb("gidx", [NR, 2, B], I32)
        gcur = [sb(f"gcur{i}", [NR, 2, BT], I32) for i in range(2)]
        ge = sb("ge", [P, BLOCK])
        dif = sb("dif", [P, 4])
        keyf = sb("keyf", [P, BLOCK, 2])
        key = sb("key", [P, BLOCK, 2], I16)
        qT = sb("qT", [P, TILES, M, P])
        qT_flat = qT[:, :, :, :].rearrange("p t m q -> p (t m q)")
        NKEY = B * BLOCK * 2
        keys = qT_flat[:, 0:NKEY // 2].bitcast(I16).rearrange("p (b o h) -> p b o h", b=B, o=BLOCK)
        eqm = qT_flat[:, NKEY // 2:NKEY].bitcast(BF16).rearrange("p (o n) -> p o n", o=BLOCK)
        idxrow = sb("idxrow", [P, 2 * B], BF16)
        last = sb("last", [P, BLOCK, 2])
        dsto = sb("dsto", [P, BLOCK, 2])
        dabs = sb("dabs", [P, 3 * BLOCK])
        sel16 = sb("sel16", [P, BLOCK])
        dst_bt = sb("dst_bt", [P, T])
        dst_it = sb("dst_it", [TILES, P])
        sidx = sb("sidx", [P, TILES], I32)
        small_i = sb("small_i", [BT, 3, TILES], I32)
        small = sb("small", [BT, 3, TILES])
        pos = sb("pos", [P, TILES])
        par = sb("par", [P, TILES])
        hi = sb("hi", [P, TILES])
        lo = sb("lo", [P, TILES])
        widx = sb("widx", [P, TILES], I32)
        mtmp = sb("mtmp", [P, 2, WIN])
        trig = sb("trig", [P, 5, TILES, HALF])
        ang, kk, red, sn, cs = (trig[:, i, :, :] for i in range(5))
        mrow = trig[:, :, :, :].rearrange("p a t d -> p (a t d)").bitcast(BF16).rearrange("p (i w) -> p i w", w=WIN)
        ccss = {w: (sb(f"cc_{w}", [P, TILES, HD]), sb(f"ss_{w}", [P, TILES, HD])) for w in "kq"}
        mask = [sb(f"mask{i}", [P, BT, WIN], BF16) for i in range(2)]
        wsg = sb("wsg", [P, TILES, HD + 1])
        xt = sb("xt", [P, 2, 2, GT * P])
        sq = sb("sq", [P, 2, GT * 2 * GH])
        ssum = sb("ssum", [P, 2, GT * 8])
        rms = sb("rms", [P, 2, GT * 8])
        rin = sb("rin", [P, 2, GT * 8])
        nrm = sb("nrm", [P, 2, GT * 2 * GH])
        ra = sb("ra", [P, 2, GT * 2 * GH])
        rb = sb("rb", [P, GT * 2 * GH])
        kvn = sb("kvn", [P, TILES, ROW])
        eqe = kvn[:, :, :].rearrange("p i c -> p (i c)")[:, 0:JW * B * NW].rearrange("p (j n) -> p j n", j=JW)
        qr = sb("qr", [P, 2, GT, M, GH])
        kv_all = sb("kv_all", [P, RING, PAIR, 2, GH])
        kv = [kv_all[:, i, :, :, :] for i in range(RING)]
        blk_st = [kv_all[:, :, :, :, :].rearrange("p r a b c -> p (r a b c)"), qT_flat[:, NKEY:NKEY + BLOCK * ROW]]
        qbd = [sb(f"qbd{i}", [P, BT, M, P]) for i in range(2)]
        kT = [sb(f"kT{i}", [P, 2, WIN]) for i in range(2)]
        sm = [sb(f"sm{i}", [P, M, WIN]) for i in range(2)]
        nmax = [sb(f"nmax{i}", [P, M]) for i in range(2)]
        pr = [sb(f"pr{i}", [P, M, WIN]) for i in range(2)]
        pT = [sb(f"pT{i}", [P, PAIR, M, P]) for i in range(2)]
        rsum = [sb(f"rsum{i}", [P, BT * M]) for i in range(2)]
        rinv = sb("rinv", [P, BT * M])
        rdiag = rb[:, 0:256].rearrange("p (a t) -> p a t", t=T)
        oT = rb[:, 256:512].rearrange("p (m b t) -> p m b t", m=M, b=BT)
        rbc = rb[:, 512:768].rearrange("p (a t) -> p a t", t=T)
        xin = [sb(f"xin{i}", [P, D]) for i in range(2)]
        x1 = [nrm[:, i, 0:D] for i in range(2)]
        ob = [nrm[:, i, D:2 * D] for i in range(2)]
        wbd = [sb(f"wbd{i}", [P, BT, HD]) for i in range(2)]

        def c(name):
            return cst[:, CO[name][0]:CO[name][1]]

        ident = c("ident")

        cst_in = sem("cst_in")
        idx_in = sem("idx_in")
        small_in = sem("small_in")
        w_in = sem("w_in")
        ent_rdy = sem("ent_rdy")
        ent_out = sem("ent_out")
        ent_in = sem("ent_in")
        blk_rdy = sem("blk_rdy")
        blk_in = [sem(f"blk_in{i}") for i in range(2)]
        blk_out = [sem(f"blk_out{i}") for i in range(2)]
        key_out = sem("key_out")
        keys_in = sem("keys_in")
        dst_out = sem("dst_out")
        dst_in = sem("dst_in")
        mask_out = sem("mask_out")
        mask_in = [sem(f"mask_in{i}") for i in range(2)]
        xt_in = [sem(f"xt_in{i}") for i in range(2)]
        chain = sem("chain")
        small_rdy = sem("small_rdy")
        small_ps = sem("small_ps")
        rows_rdy = sem("rows_rdy")
        rows_ps = sem("rows_ps")
        gidx_rdy = sem("gidx_rdy")
        key_rdy = sem("key_rdy")
        dst_rdy = sem("dst_rdy")
        dst_ps = sem("dst_ps")
        sidx_rdy = sem("sidx_rdy")
        widx_rdy = sem("widx_rdy")
        ws_in = sem("ws_in")
        mask_rdy = sem("mask_rdy")
        ang_rdy = sem("ang_rdy")
        sin_done = sem("sin_done")
        rope_rdy = sem("rope_rdy")
        zeroed = sem("zeroed")
        proj_done = sem("proj_done")
        sq_done = sem("sq_done")
        ss_done = sem("ss_done")
        rms_done = sem("rms_done")
        rin_done = sem("rin_done")
        nrm_done = sem("nrm_done")
        vcopy = sem("vcopy")
        ra_done = sem("ra_done")
        rb_done = sem("rb_done")
        rope_done = sem("rope_done")
        qt_ps = sem("qt_ps")
        qt_done = sem("qt_done")
        scat = sem("scat")
        old_in = [sem(f"old_in{i}") for i in range(RING)]
        win_in = [sem(f"win_in{i}") for i in range(RING)]
        gcur_done = sem("gcur_done")
        pool_passed = sem("pool_passed")
        dve_passed = sem("dve_passed")
        kt_ps = sem("kt_ps")
        kt_done = sem("kt_done")
        s_done = sem("s_done")
        sm_done = sem("sm_done")
        exp_done = sem("exp_done")
        pt_ps = sem("pt_ps")
        pt_done = sem("pt_done")
        pv_done = sem("pv_done")
        rinv_done = sem("rinv_done")
        rdiag_done = sem("rdiag_done")
        r_done = sem("r_done")
        rbc_done = sem("rbc_done")
        on_done = sem("on_done")
        wo_done = sem("wo_done")
        x1_done = sem("x1_done")
        l1_done = sem("l1_done")
        ob_done = sem("ob_done")
        qbd_done = sem("qbd_done")
        wbd_done = sem("wbd_done")
        x_in = [sem(f"x_in{i}") for i in range(2)]
        o_out = [sem(f"o_out{i}") for i in range(2)]

        block = ctx.enter_context(nc.Block())
        NB1 = 2 * NGRP

        def alone(eng, sem_):
            eng.sem_inc(sem_, 1)

        def runs(emit):
            def driver(eng):
                emit(0, True, False)
                with eng.Fori(1, B // 8 - 1) as it:
                    emit(it, False, False)
                emit(B // 8 - 1, False, True)
            return driver

        @block.sync
        def _(sp):
            sp.dma_start(cst[:, :], consts).then_inc(cst_in, 16)
            sp.dma_start(tab_i[:, :], table).then_inc(idx_in, 16)
            sp.dma_start(p0_i[:, 0:1], p0.rearrange("(b o) -> b o", o=1)).then_inc(idx_in, 16)
            sp.dma_start(small_i[:, 0, :], p0T).then_inc(small_in, 16)
            sp.dma_start(small_i[:, 2, :], subjT).then_inc(small_in, 16)
            sp.dma_start(sel4_sb[:, :], sel4).then_inc(small_in, 16)
            sp.dma_start(wkv[:, :, :], wkvT.rearrange("(c p) n -> p c n", p=P)).then_inc(w_in, 16)
            sp.dma_start(wq[:, :, :], wqT.rearrange("(c p) n -> p c n", p=P)).then_inc(w_in, 16)
            sp.dma_start(wo[:, :, :], woT.rearrange("(m p) n -> p m n", p=P)).then_inc(w_in, 16)
            sp.dma_start(qs_sb[:, :], qs.partition_broadcast(P)).then_inc(w_in, 16)
            sp.dma_start(ks_sb[:, :], ks.partition_broadcast(P)).then_inc(w_in, 16)

            xT_v = xT.rearrange("(c p) n -> p c n", p=P)

            def load_xt(grp, k, waits):
                if waits is not None:
                    sp.wait_ge(proj_done, waits)
                sp.dma_start(xt[:, k, :, :], xT_v[:, :, bass.ts(grp, GT * P)]).then_inc(xt_in[k], 16)

            for k in range(2):
                load_xt(k, k, None)
            sp.wait_ge(ent_rdy, 1)
            sp.dma_start(ent_dram, blkw[:, JW - NW:JW]).then_inc(ent_out, 16)
            sp.wait_ge(ent_out, 16)
            sp.dma_start(ents[:, :], ent_dram.rearrange("b k -> (b k)").partition_broadcast(P)).then_inc(ent_in, 16)
            merged_b = merged.rearrange("(b w o) c -> b w (o c)", w=NW, o=BLOCK)
            for w in range(NW):
                sp.wait_ge(blk_in[w % 2], 16 * (w // 2 + 1))
                sp.dma_start(merged_b[:, w, :], blk_st[w % 2]).then_inc(blk_out[w % 2], 16)
            sp.wait_ge(key_rdy, 1)
            sp.dma_start(key_dram, key[:, :, :].rearrange("p a b -> p (a b)")).then_inc(key_out, 16)
            sp.wait_ge(key_out, 16)
            sp.dma_start(keys[:, :, :, :].rearrange("p b o h -> p (b o h)"),
                         key_dram.rearrange("b k -> (b k)").partition_broadcast(P)).then_inc(keys_in, 16)
            for p_ in range(2):
                with sp.Fori(1 - p_, NGRP // 2) as it:
                    for k in range(2):
                        load_xt(it * 2 + k, k, it * 4 + (p_ * NB1 + 2 * k - 2))
                if p_ == 0:
                    sp.wait_ge(dst_rdy, 1)
                    sp.dma_start(dst_dram, dst_bt[:, :]).then_inc(dst_out, 16)
                    sp.wait_ge(dst_out, 16)
                    sp.dma_start(dst_it[:, :], dst_dram.rearrange("(i q) t -> i (q t)", q=BT)).then_inc(dst_in, 16)
            sp.wait_ge(mask_rdy, 1)
            for q in range(BT):
                sp.dma_start(mask_dram[:, :, q, :].rearrange("i t w -> t i w"), mrow[q * T:(q + 1) * T, :, :])\
                    .then_inc(mask_out, 16)
            sp.wait_ge(mask_out, 16 * BT)

            def load_mask(tile, k):
                for g in range(G):
                    sp.dma_start(mask[k][g * T:(g + 1) * T, :, :].rearrange("t q w -> t (q w)"),
                                 mask_dram[bass.ds(tile, 1), :, :, :].rearrange("i t q w -> (i t) (q w)"))\
                        .then_inc(mask_in[k], 16)

            def load_x(tile, k):
                sp.dma_start(xin[k][:, :], x[bass.ts(tile, P), :]).then_inc(x_in[k], 16)

            def step(it, first, last_):
                for k in range(2):
                    tile = it * 2 + k
                    if not last_:
                        sp.wait_ge(sm_done, tile * 4 + 4)
                        load_mask(tile + 2, k)
                        sp.wait_ge(x1_done, tile + 1)
                        load_x(tile + 2, k)
                    sp.wait_ge(ob_done, tile + 1)
                    sp.dma_start(out[bass.ts(tile, P), :], ob[k][:, :]).then_inc(o_out[k], 16)

            for k in range(2):
                load_mask(k, k)
                load_x(k, k)
            runs(step)(sp)
            for k in range(2):
                sp.wait_ge(o_out[k], 16 * (TILES // 2))

        @block.gpsimd
        def _(pool):
            pool.wait_ge(blk_rdy, 1)
            for w in range(NW):
                if w >= 2:
                    pool.wait_ge(blk_out[w % 2], 16)
                pool.indirect_dma_start(blk_st[w % 2], None, cache.rearrange("(r a) c -> r (a c)", a=BLOCK),
                                        bass.IndirectOffsetOnAxis(ap=blk_i[:, w:w + 1], axis=0),
                                        bounds_check=CBLK - 1, oob_is_err=False).then_inc(blk_in[w % 2], 16)
            for i in range(2):
                pool.memset(qbd[i][:, :, :, :], 0.0).then_inc(zeroed, 1)
                pool.wait_ge(zeroed, 2 * i + 1)
                pool.memset(pT[i][64:P, :, :, :], 0.0).then_inc(zeroed, 1)
                pool.wait_ge(zeroed, 2 * i + 2)

            pool.wait_ge(widx_rdy, 1)
            for i in range(TILES):
                pool.indirect_dma_start(wsg[:, i, :], None, wsub,
                                        bass.IndirectOffsetOnAxis(ap=widx[:, i:i + 1], axis=0),
                                        bounds_check=NSUB * HD - 1, oob_is_err=False).then_inc(ws_in, 16)

            def rope_a(grp, k, w, heads, cnt):
                pool.wait_ge(nrm_done, cnt + 1)
                n = GT * heads * HD
                a = nrm[:, k, 0:n].rearrange("p (t h d) -> p t h d", t=GT, h=heads)
                cc = ccss[w][0][:, bass.ts(grp, GT), :].rearrange("p t (o d) -> p t o d", o=1).broadcast_to([P, GT, heads, HD])
                pool.tensor_tensor(ra[:, k, 0:n].rearrange("p (t h d) -> p t h d", t=GT, h=heads), a, cc, ALU.mult)\
                    .then_inc(ra_done, 1)

            pool.wait_ge(rope_rdy, 1)
            for grp in range(NGRP):
                if grp >= 2:
                    pool.wait_ge(rope_done, grp - 1)
                rope_a(grp, grp % 2, "k", G, grp)
            pool.wait_ge(blk_out[0], 32)
            pool.wait_ge(blk_out[1], 16)
            pool.wait_ge(ra_done, NGRP)
            pool.memset(kv_all[64:P, :, :, :, :], 0.0).then_inc(zeroed, 1)
            pool.wait_ge(zeroed, 5)
            pool.wait_ge(sidx_rdy, 1)
            for grp in range(NGRP):
                pool.wait_ge(rope_done, grp + 1)
                pool.wait_ge(vcopy, 2 * grp + 2)
                for i in range(grp * GT, (grp + 1) * GT):
                    pool.indirect_dma_start(merged, bass.IndirectOffsetOnAxis(ap=sidx[:, i:i + 1], axis=0),
                                            kvn[:, i, :], None,
                                            bounds_check=B * NW * BLOCK - 1, oob_is_err=False).then_inc(scat, 16)
                pool.wait_ge(rope_done, NGRP + grp - 1)
                rope_a(grp, grp % 2, "q", 2 * G, NGRP + grp)

            def gather_old(index, k):
                pool.indirect_dma_start(kv[k][0:NR, :, :, :].rearrange("p a b c -> p (a b c)"), None,
                                        cache.rearrange("(r a) c -> r (a c)", a=PAIR),
                                        bass.IndirectOffsetOnAxis(ap=index, axis=0),
                                        bounds_check=CBLK * RB - 1, oob_is_err=False).then_inc(old_in[k], 16)

            def gather_new(index, k):
                pool.indirect_dma_start(kv[k][0:NR, :, :, :].rearrange("p a b c -> p (a b c)"), None,
                                        merged.rearrange("(r a) c -> r (a c)", a=PAIR),
                                        bass.IndirectOffsetOnAxis(ap=index, axis=0),
                                        bounds_check=B * NW * RB - 1, oob_is_err=False).then_inc(win_in[k], 16)

            pool.wait_ge(gidx_rdy, 1)
            pool.wait_ge(zeroed, 5)
            for n in range(RING):
                gather_old(gidx[:, 0, n:n + 1], n)
            pool.wait_ge(scat, 16 * TILES)
            for n in range(RING):
                pool.wait_ge(old_in[n], 16)
                gather_new(gidx[:, 1, n:n + 1], n)

            def step(it, first, last_):
                for k in range(2):
                    tile = it * 2 + k
                    if last_:
                        continue
                    for j in range(4):
                        pool.wait_ge(win_in[4 * k + j], 16 * (it + 1))
                    pool.tensor_copy(gcur[k][:, :, :], gidx[:, :, bass.ds(tile * 4 + RING, 4)]).then_inc(gcur_done, 1)
                    pool.wait_ge(gcur_done, tile + 1)
                    for src, j in ((0, 0), (0, 1), (1, 0), (0, 2), (1, 1), (0, 3), (1, 2), (1, 3)):
                        if src == 0:
                            pool.wait_ge(pv_done, tile * 4 + (j + 1))
                            alone(pool, pool_passed)
                            gather_old(gcur[k][:, 0, j:j + 1], 4 * k + j)
                        else:
                            pool.wait_ge(old_in[4 * k + j], 16 * (it + 2))
                            alone(pool, pool_passed)
                            gather_new(gcur[k][:, 1, j:j + 1], 4 * k + j)

            runs(step)(pool)

        @block.scalar
        def _(act):
            act.wait_ge(ang_rdy, 1)
            nc.scalar.activation(sn[:, :, :], red[:, :, :], ACT.Sin).then_inc(sin_done, 1)
            act.wait_ge(ang_rdy, 2)
            nc.scalar.activation(cs[:, :, :], kk[:, :, :], ACT.Sin).then_inc(sin_done, 1)
            act.wait_ge(cst_in, 16)

            def root(grp_cnt, k, n):
                act.wait_ge(ss_done, grp_cnt + 1)
                nc.scalar.activation(rms[:, k, 0:n], ssum[:, k, 0:n], ACT.Sqrt, bias=c("eps"), scale=1.0 / HD)\
                    .then_inc(rms_done, 1)

            def squares(pss, grp_cnt, k, first):
                for h in range(2):
                    act.wait_ge(proj_done, grp_cnt * 2 + (h + 1))
                    if h == 0 and not first:
                        act.wait_ge(ss_done, grp_cnt - 1)
                    src = bank[2 * k + h][:, :].rearrange("p (t n) -> p t n", t=2)
                    if pss == 0:
                        nc.scalar.activation(sq[:, k, h * 2 * GH:(h + 1) * 2 * GH].rearrange("p (t n) -> p t n", t=2),
                                             src[:, :, 0:GH], ACT.Square).then_inc(sq_done, 1)
                    else:
                        nc.scalar.activation(sq[:, k, h * 4 * GH:(h + 1) * 4 * GH], bank[2 * k + h][:, :], ACT.Square)\
                            .then_inc(sq_done, 1)

            def values(grp, k):
                if grp == 0:
                    act.wait_ge(rows_rdy, 1)
                for h in range(2):
                    src = bank[2 * k + h][:, :].rearrange("p (t n) -> p t n", t=2)
                    nc.scalar.activation(kvn[:, bass.ds(grp * GT + 2 * h, 2), GH:ROW], src[:, :, GH:2 * GH], ACT.Copy)\
                        .then_inc(vcopy, 1)

            for grp in range(NGRP):
                squares(0, grp, grp % 2, grp < 2)
                values(grp, grp % 2)
                root(grp, grp % 2, GT * G)

            def evac(grp):
                if grp == 0:
                    act.wait_ge(dst_rdy, 1)
                for h in range(2):
                    act.wait_ge(qt_ps, 2 * grp + h + 1)
                    nc.scalar.activation(qT[:, bass.ds(grp * GT + 2 * h, 2), :, :].rearrange("p t m q -> p (t m q)"),
                                         bank[4 + h][:, :], ACT.Copy).then_inc(qt_done, 1)

            for grp in range(NGRP):
                squares(1, NGRP + grp, grp % 2, False)
                root(NGRP + grp, grp % 2, GT * 2 * G)
                if grp >= 1:
                    evac(grp - 1)
            evac(NGRP - 1)

            def kt_evac(m, k):
                act.wait_ge(kt_ps, m + 1)
                nc.scalar.activation(kT[k][:, :, :].rearrange("p b (e n) -> p (b e) n", e=PAIR),
                                     bank[4][:, :].rearrange("p (b n) -> p b n", b=4)[:, :, 0:NR],
                                     ACT.Copy).then_inc(kt_done, 1)

            def make_qbd(tile, k):
                for g in range(G):
                    ins = nc.scalar.activation(qbd[k][g * HD:(g + 1) * HD, :, :, g * T:(g + 1) * T],
                                           qT[g * HD:(g + 1) * HD, bass.ds(tile, 1), :, :].rearrange(
                                               "p o m (q t) -> p (o q) m t", q=BT), ACT.Copy)
                    if g == G - 1:
                        ins.then_inc(qbd_done, 1)

            act.wait_ge(zeroed, 5)
            act.wait_ge(qt_done, NB1)
            make_qbd(0, 0)
            kt_evac(0, 0)

            def step(it, first, last_):
                for j in range(8):
                    if j % 4 == 1 and not (last_ and j == 5):
                        if not (first and j == 1):
                            act.wait_ge(s_done, it * 8 + (j - 1))
                        make_qbd(it * 2 + (j // 4 + 1), (j // 4 + 1) % 2)
                    n = it * 8 + j
                    b2 = j % 2
                    act.wait_ge(sm_done, n + 1)
                    if not (first and j < 2):
                        act.wait_ge(pt_ps, n - 1)
                    if j % 4 == 0 and not first:
                        act.wait_ge(rinv_done, it * 2 + (j // 4 - 1))
                    for m in range(M):
                        col = (j % 4) * M + m
                        ins = nc.scalar.activation(pr[b2][:, m, :], sm[b2][:, m, :], ACT.Exp,
                                                   bias=nmax[b2][:, m:m + 1], scale=-1.0,
                                                   accum_out=rsum[j // 4][:, col:col + 1])
                    ins.then_inc(exp_done, 1)
                    if j % 2 == 0 and not (last_ and j == 6):
                        if not (first and j == 0):
                            act.wait_ge(s_done, n)
                        kt_evac(it * 4 + (j // 2 + 1), (j // 2 + 1) % 2)

            runs(step)(act)

        @block.vector
        def _(dve):
            n_chain = [0]

            def link(ins):
                n_chain[0] += 1
                ins.then_inc(chain, 1)
                dve.wait_ge(chain, n_chain[0])

            V = nc.vector
            dve.wait_ge(cst_in, 16)
            dve.wait_ge(small_in, 48)
            link(V.tensor_scalar(small_i[:, 1, :], small_i[:, 0, :], 1, None, ALU.bitwise_and))
            V.tensor_copy(small[:, :, :], small_i[:, :, :]).then_inc(small_rdy, 1)
            dve.wait_ge(small_ps, 1)
            ps = bank[6]
            V.tensor_scalar(par[:, :], ps[:, TILES:2 * TILES], 1.0, None, ALU.mult)
            V.tensor_scalar(widx[:, :], ps[:, 2 * TILES:3 * TILES], float(HD), c("tcol"), ALU.mult, ALU.add)\
                .then_inc(widx_rdy, 1)
            V.tensor_scalar(lo[:, :], ps[:, 0:TILES], -1.0, 128.0, ALU.mult, ALU.add)
            link(V.tensor_scalar(pos[:, :], ps[:, 0:TILES], c("tcol"), None, ALU.add))
            pos_b = pos[:, :].rearrange("p (t o) -> p t o", o=1).broadcast_to([P, TILES, HALF])
            inv_b = c("inv").rearrange("p (o d) -> p o d", o=1).broadcast_to([P, TILES, HALF])
            link(V.tensor_tensor(ang[:, :, :], pos_b, inv_b, ALU.mult))

            def reduced(dest, shift):
                link(V.tensor_scalar(kk[:, :, :], ang[:, :, :], INV2PI, shift / (2 * 3.141592653589793), ALU.mult, ALU.add))
                link(V.tensor_scalar(kk[:, :, :], kk[:, :, :], MAGIC, None, ALU.add))
                link(V.tensor_scalar(kk[:, :, :], kk[:, :, :], MAGIC, None, ALU.subtract))
                link(V.scalar_tensor_tensor(dest[:, :, :], kk[:, :, :], -TWO_PI[0], ang[:, :, :], ALU.mult, ALU.add))
                link(V.scalar_tensor_tensor(dest[:, :, :], kk[:, :, :], -TWO_PI[1], dest[:, :, :], ALU.mult, ALU.add))
                link(V.scalar_tensor_tensor(dest[:, :, :], kk[:, :, :], -TWO_PI[2], dest[:, :, :], ALU.mult, ALU.add))

            reduced(red, 0.0)
            link(V.tensor_scalar(red[:, :, :], red[:, :, :], PI_IN, -PI_IN, ALU.min, ALU.max))
            dve.sem_inc(ang_rdy, 1)
            reduced(cs, HALF_PI)
            link(V.tensor_scalar(cs[:, :, :], cs[:, :, :], HALF_PI, PI_IN, ALU.add, ALU.min))
            V.tensor_scalar(kk[:, :, :], cs[:, :, :], -PI_IN, None, ALU.max).then_inc(ang_rdy, 1)

            dve.wait_ge(idx_in, 32)
            V.tensor_copy(tab[:, :], tab_i[:, :])
            V.tensor_scalar(p0_i[:, 1:2], p0_i[:, 0:1], 4, None, ALU.arith_shift_right)
            link(V.tensor_scalar(p0_i[:, 2:3], p0_i[:, 0:1], BLOCK - 1, None, ALU.bitwise_and))
            V.tensor_copy(pra[:, 0:1], p0_i[:, 2:3])
            V.tensor_copy(pra[:, 1:2], p0_i[:, 1:2])
            link(V.tensor_scalar(p0_i[:, 0:1], p0_i[:, 2:3], 1, None, ALU.add))
            link(V.tensor_scalar(p0_i[:, 0:1], p0_i[:, 0:1], 1, None, ALU.arith_shift_right))
            V.tensor_copy(pra[:, 2:3], p0_i[:, 0:1])
            link(V.tensor_scalar(slot[:, :], c("jwin"), pra[:, 1:2], 0.0, ALU.add, ALU.max))
            link(V.tensor_scalar(slot[:, :], slot[:, :], float(NBLK - 1), None, ALU.min))
            for j in range(JW):
                link(V.scalar_tensor_tensor(junk[:, :], c("iota"), slot[:, j:j + 1], tab[:, :], ALU.is_equal, ALU.mult,
                                            accum_out=blkw[:, j:j + 1]))
            dve.sem_inc(ent_rdy, 1)
            V.tensor_copy(blk_i[:, :], blkw[:, JW - NW:JW]).then_inc(blk_rdy, 1)
            r = pra[:, 0:1]
            T0, T1, T2 = (blkw[:, 8 + w:9 + w] for w in range(3))
            V.tensor_scalar(ge[:, :], c("iota")[:, 0:BLOCK], r, None, ALU.is_ge)
            V.tensor_tensor(dif[:, 0:1], T0, T1, ALU.subtract)
            link(V.tensor_tensor(dif[:, 1:2], T1, T2, ALU.subtract))
            V.tensor_scalar(keyf[:, :, 0], ge[:, :], dif[:, 0:1], T1, ALU.mult, ALU.add)
            link(V.tensor_scalar(keyf[:, :, 1], ge[:, :], dif[:, 1:2], T2, ALU.mult, ALU.add))
            V.tensor_copy(key[:, :, :], keyf[:, :, :]).then_inc(key_rdy, 1)
            dve.wait_ge(key_rdy, 1)
            dve.wait_ge(ent_in, 16)
            link(V.tensor_tensor(eqe, ents[:, :].rearrange("p (o n) -> p o n", o=1).broadcast_to([P, JW, B * NW]),
                                 blkw[:, :].rearrange("p (j o) -> p j o", o=1).broadcast_to([P, JW, B * NW]), ALU.is_equal))
            link(V.tensor_tensor(eqe, eqe, c("idxrow").rearrange("p (o n) -> p o n", o=1).broadcast_to([P, JW, B * NW]),
                                 ALU.mult))
            link(V.tensor_reduce(repb[:, :], eqe, AX, ALU.max))
            V.tensor_scalar(hit[:, 0, :], repb[:, :], 0.0, MISS, ALU.is_gt, ALU.mult)
            link(V.tensor_scalar(hit[:, 1, :], repb[:, :], 0.0, MISS, ALU.is_equal, ALU.mult))
            V.scalar_tensor_tensor(hit[:, 0, :], blkw[:, :], float(RB), hit[:, 0, :], ALU.mult, ALU.add)
            link(V.scalar_tensor_tensor(hit[:, 1, :], repb[:, :], float(RB), hit[:, 1, :], ALU.mult, ALU.add))
            link(V.tensor_scalar(hit[:, 1, :], hit[:, 1, :], -float(RB), None, ALU.add))
            o_b = c("oprow").rearrange("p (o r) -> p o r", o=1).broadcast_to([P, JW, RB])
            for s_ in range(2):
                V.tensor_tensor(rows88[:, s_, :].rearrange("p (j o) -> p j o", j=JW),
                                hit[:, s_, :].rearrange("p (j o) -> p j o", o=1).broadcast_to([P, JW, RB]), o_b, ALU.add)
            link(V.tensor_scalar(sel9[:, :], c("iota")[:, 0:RB + 1], pra[:, 2:3], None, ALU.is_equal))
            link(V.tensor_scalar(rows[:, :, :], rows88[:, :, 0:NR], sel9[:, 0:1], None, ALU.mult))
            for v in range(1, RB + 1):
                ins = V.scalar_tensor_tensor(rows[:, :, :], rows88[:, :, v:v + NR], sel9[:, v:v + 1], rows[:, :, :],
                                             ALU.mult, ALU.add)
                if v < RB:
                    link(ins)
            ins.then_inc(rows_rdy, 1)
            dve.wait_ge(rows_ps, 1)
            V.tensor_copy(gidx[:, :, :].rearrange("p s b -> p (s b)"), bank[7][0:NR, 0:2 * B]).then_inc(gidx_rdy, 1)
            R0, R1, R2 = (repb[:, 8 + w:9 + w] for w in range(3))
            V.tensor_tensor(dif[:, 2:3], R0, R1, ALU.subtract)
            link(V.tensor_tensor(dif[:, 3:4], R1, R2, ALU.subtract))
            V.tensor_scalar(keyf[:, :, 0], ge[:, :], dif[:, 2:3], R1, ALU.mult, ALU.add)
            link(V.tensor_scalar(keyf[:, :, 1], ge[:, :], dif[:, 3:4], R2, ALU.mult, ALU.add))
            link(V.tensor_scalar(keyf[:, :, :], keyf[:, :, :], -1.0, float(BLOCK), ALU.add, ALU.mult))

            dve.wait_ge(w_in, 80)
            dve.wait_ge(sin_done, 2)
            for sc_ in (qs_sb, ks_sb):
                link(V.tensor_scalar(sc_[:, :], sc_[:, :], 1.0, None, ALU.add))
            for w, sc_ in (("k", ks_sb), ("q", qs_sb)):
                cc, ss = ccss[w]
                lo_b, hi_b = (sc_[:, h * HALF:(h + 1) * HALF].rearrange("p (o d) -> p o d", o=1)
                              .broadcast_to([P, TILES, HALF]) for h in range(2))
                V.tensor_tensor(cc[:, :, 0:HALF], cs[:, :, :], lo_b, ALU.mult)
                V.tensor_tensor(cc[:, :, HALF:HD], cs[:, :, :], hi_b, ALU.mult)
                V.scalar_tensor_tensor(ss[:, :, 0:HALF], sn[:, :, :], -1.0, hi_b, ALU.mult, ALU.mult)
                ins = V.tensor_tensor(ss[:, :, HALF:HD], sn[:, :, :], lo_b, ALU.mult)
            ins.then_inc(rope_rdy, 1)
            dve.wait_ge(rope_rdy, 1)

            link(V.tensor_copy(idxrow[:, :], c("idxrow")[:, 0:2 * B]))
            dve.wait_ge(keys_in, 16)
            for h in range(2):
                mine = key[:, :, h:h + 1].rearrange("p o (a z) -> p o a z", a=1).broadcast_to([P, BLOCK, B, 2])
                link(V.tensor_tensor(eqm[:, :, :].rearrange("p o (b h) -> p o b h", h=2),
                                     keys[:, :, :, :].rearrange("p b o h -> p o b h"), mine, ALU.is_equal))
                link(V.tensor_tensor(eqm[:, :, :], eqm[:, :, :],
                                     idxrow[:, :].rearrange("p (o n) -> p o n", o=1).broadcast_to([P, BLOCK, 2 * B]), ALU.mult))
                link(V.tensor_reduce(last[:, :, h], eqm[:, :, :], AX, ALU.max))
                V.tensor_tensor(dsto[:, :, h], keyf[:, :, h], c("iota")[:, 0:BLOCK], ALU.add)
                link(V.tensor_scalar(last[:, :, h], last[:, :, h], c("own")[:, h:h + 1], MISS, ALU.not_equal, ALU.mult))
                link(V.tensor_tensor(dsto[:, :, h], dsto[:, :, h], last[:, :, h], ALU.add))
            V.tensor_copy(dabs[:, 0:BLOCK], dsto[:, :, 0])
            V.tensor_copy(dabs[:, 2 * BLOCK:3 * BLOCK], dsto[:, :, 1])
            V.tensor_scalar(sel16[:, :], c("iota")[:, 0:BLOCK], r, None, ALU.is_equal)
            link(V.tensor_tensor(last[:, :, 0], dsto[:, :, 1], dsto[:, :, 0], ALU.subtract))
            link(V.tensor_tensor(last[:, :, 0], last[:, :, 0], ge[:, :], ALU.mult))
            link(V.tensor_tensor(dabs[:, BLOCK:2 * BLOCK], last[:, :, 0], dsto[:, :, 0], ALU.add))
            link(V.tensor_scalar(dst_bt[:, :], dabs[:, 0:T], sel16[:, 0:1], None, ALU.mult))
            for v in range(1, BLOCK):
                ins = V.scalar_tensor_tensor(dst_bt[:, :], dabs[:, v:v + T], sel16[:, v:v + 1], dst_bt[:, :], ALU.mult, ALU.add)
                if v < BLOCK - 1:
                    link(ins)
            ins.then_inc(dst_rdy, 1)

            def norm(pss, grp_cnt, k, w, heads, grp):
                n = GT * heads * HD
                dve.wait_ge(sq_done, 2 * grp_cnt + 2)
                V.tensor_reduce(ssum[:, k, 0:GT * heads], sq[:, k, 0:n].rearrange("p (a d) -> p a d", d=HD), AX, ALU.add)\
                    .then_inc(ss_done, 1)
                dve.wait_ge(rms_done, grp_cnt + 1)
                V.reciprocal(rin[:, k, 0:GT * heads], rms[:, k, 0:GT * heads]).then_inc(rin_done, 1)
                dve.wait_ge(rin_done, grp_cnt + 1)
                for h in range(2):
                    src = bank[2 * k + h][:, :].rearrange("p (t a d) -> p t a d", t=2, d=HD)[:, :, 0:heads, :]
                    rv = rin[:, k, h * 2 * heads:(h + 1) * 2 * heads].rearrange("p (t a o) -> p t a o", t=2, o=1)\
                        .broadcast_to([P, 2, heads, HD])
                    ins = V.tensor_tensor(nrm[:, k, h * n // 2:(h + 1) * n // 2].rearrange("p (t a d) -> p t a d", t=2, d=HD),
                                          src, rv, ALU.mult)
                ins.then_inc(nrm_done, 1)
                dve.wait_ge(nrm_done, grp_cnt + 1)
                v4 = nrm[:, k, 0:n].rearrange("p (t a d) -> p t a d", t=GT, d=HD)
                o4 = rb[:, 0:n].rearrange("p (t a d) -> p t a d", t=GT, d=HD)
                ss = ccss[w][1][:, grp * GT:(grp + 1) * GT, :].rearrange("p t (o d) -> p t o d", o=1)
                for h in range(2):
                    ins = V.tensor_tensor(o4[:, :, :, h * HALF:(h + 1) * HALF], v4[:, :, :, (1 - h) * HALF:(2 - h) * HALF],
                                          ss[:, :, :, h * HALF:(h + 1) * HALF].broadcast_to([P, GT, heads, HALF]), ALU.mult)
                ins.then_inc(rb_done, 1)
                dve.wait_ge(rb_done, grp_cnt + 1)
                dve.wait_ge(ra_done, grp_cnt + 1)
                if pss == 0:
                    dest = kvn[:, grp * GT:(grp + 1) * GT, 0:GH]
                else:
                    if grp >= 2:
                        dve.wait_ge(qt_ps, 2 * grp - 2)
                    dest = qr[:, k, :, :, :].rearrange("p t m q -> p t (m q)")
                V.tensor_tensor(dest, ra[:, k, 0:n].rearrange("p (t n) -> p t n", t=GT),
                                rb[:, 0:n].rearrange("p (t n) -> p t n", t=GT), ALU.add).then_inc(rope_done, 1)

            for grp in range(NGRP):
                norm(0, grp, grp % 2, "k", G, grp)
            dve.wait_ge(dst_ps, 1)
            V.tensor_copy(sidx[:, :], bank[6][:, 128:128 + TILES]).then_inc(sidx_rdy, 1)
            for grp in range(NGRP):
                norm(1, NGRP + grp, grp % 2, "q", 2 * G, grp)

            link(V.tensor_tensor(lo[:, :], lo[:, :], par[:, :], ALU.subtract))
            V.tensor_scalar(hi[:, :], par[:, :], -1.0, c("tcol"), ALU.mult, ALU.add)
            link(V.tensor_scalar(par[:, :], par[:, :], -1.0, c("tcol"), ALU.mult, ALU.add))
            link(V.tensor_scalar(hi[:, :], hi[:, :], 128.0, None, ALU.add))
            link(V.tensor_scalar(par[:, :], par[:, :], 1.0, None, ALU.add))
            link(V.tensor_tensor(lo[:, :], lo[:, :], par[:, :], ALU.max))
            for i in range(TILES):
                k = i % 2
                link(V.tensor_scalar(mtmp[:, k, :], c("upos"), hi[:, i:i + 1], -1.0, ALU.subtract, ALU.mult))
                link(V.scalar_tensor_tensor(mrow[:, i, :], c("upos"), lo[:, i:i + 1], mtmp[:, k, :], ALU.subtract, ALU.min))
            V.tensor_scalar(mrow[:, :, :], mrow[:, :, :], 0.0, BIG, ALU.min, ALU.mult).then_inc(mask_rdy, 1)

            def pt_evac(n, k, free):
                dve.wait_ge(pt_ps, n + 1)
                if free is not None:
                    dve.wait_ge(pv_done, free)
                V.tensor_copy(pT[k][0:NR, :, :, :].rearrange("p e m q -> p (e m q)"), bank[2 + k][0:NR, :])\
                    .then_inc(pt_done, 1)

            def diag(tile, k):
                dve.wait_ge(exp_done, tile * 4 + 4)
                V.reciprocal(rinv[:, :], rsum[k][:, :]).then_inc(rinv_done, 1)
                dve.wait_ge(rinv_done, tile + 1)
                V.tensor_tensor(rdiag[:, :, :], c("dmask").rearrange("p (o t) -> p o t", o=1).broadcast_to([P, BT * M, T]),
                                rinv[:, :].rearrange("p (n o) -> p n o", o=1).broadcast_to([P, BT * M, T]), ALU.mult)\
                    .then_inc(rdiag_done, 1)

            def rbc_copy(tile):
                dve.wait_ge(pv_done, tile * 4 + 4)
                dve.wait_ge(r_done, tile + 1)
                V.tensor_copy(rbc[:, :, :].rearrange("p a t -> p (a t)"), bank[5][:, 256:512]).then_inc(rbc_done, 1)

            def normed(tile, k, wait_wo):
                rbc_copy(tile)
                dve.wait_ge(rbc_done, tile + 1)
                if wait_wo:
                    dve.wait_ge(wo_done, tile)
                V.tensor_tensor(oT[:, :, :, :].rearrange("p m b t -> p b m t"),
                                bank[5][:, 0:256].rearrange("p (b m t) -> p b m t", b=BT, m=M),
                                rbc[:, :, :].rearrange("p (b m) t -> p b m t", b=BT), ALU.mult).then_inc(on_done, 1)

            def residual(tile, k, it2):
                dve.wait_ge(wo_done, tile + 1)
                dve.wait_ge(x_in[k], it2)
                V.tensor_tensor(x1[k][:, :], bank[6][:, 0:D], xin[k][:, :], ALU.add).then_inc(x1_done, 1)

            def result(tile, k, stored):
                dve.wait_ge(l1_done, tile + 1)
                if stored is not None:
                    dve.wait_ge(o_out[k], stored)
                V.scalar_tensor_tensor(ob[k][:, :], bank[7][:, 0:D], wsg[:, bass.ds(tile, 1), HD:HD + 1].rearrange("p o d -> p (o d)"),
                                       x1[k][:, :], ALU.add, ALU.add).then_inc(ob_done, 1)

            def step(it, first, last_):
                for j in range(8):
                    n = it * 8 + j
                    b2 = j % 2
                    if j % 4 == 0:
                        dve.wait_ge(mask_in[j // 4], it * 64 + 64)
                    dve.wait_ge(s_done, n + 1)
                    if not (first and j < 2):
                        dve.wait_ge(exp_done, n - 1)
                    alone(dve, dve_passed)
                    for m in range(M):
                        ins = V.tensor_tensor_reduce(out=sm[b2][:, m, :], in0=bank[b2][:, m * WIN:(m + 1) * WIN],
                                                     in1=mask[j // 4][:, j % 4, :],
                                                     scale=-SCALE, scalar=3.0e38, op0=ALU.add, op1=ALU.min,
                                                     accum_out=nmax[b2][:, m:m + 1])
                    ins.then_inc(sm_done, 1)
                    tl = it * 2 + (j // 4 - 1)
                    tk = (j // 4 + 1) % 2
                    tail = not (first and j < 4)
                    if j % 4 == 0 and tail:
                        diag(tl, tk)
                    if not (first and j == 0):
                        pt_evac(n - 1, (j - 1) % 2, None if first and j <= 2 else n - 2)
                    if not tail or j % 4 == 0:
                        continue
                    if j % 4 == 1:
                        make_wbd(tl, tk, not (isinstance(it, int) and tl <= 1))
                        normed(tl, tk, not (first and j < 8 and j // 4 == 1))
                    elif j % 4 == 2:
                        residual(tl, tk, 16 * (it + 1) if j > 4 else 16 * it)
                    else:
                        result(tl, tk, None if first else (16 * it if j > 4 else 16 * (it - 1)) if not isinstance(it, int)
                               else max(0, 16 * it if j > 4 else 16 * (it - 1)) or None)

            def make_wbd(tile, k, used):
                if used:
                    dve.wait_ge(l1_done, tile - 1)
                w = wsg[:, bass.ds(tile, 1), 0:HD].broadcast_to([P, BT, HD])
                m = c("bdm").rearrange("p (q o) -> p q o", o=1).broadcast_to([P, BT, HD])
                V.tensor_tensor(wbd[k][:, :, :], w, m, ALU.mult).then_inc(wbd_done, 1)

            dve.wait_ge(zeroed, 5)
            dve.wait_ge(ws_in, 16 * TILES)
            step(0, True, False)
            step(1, False, False)
            with dve.Fori(2, B // 8) as it:
                step(it, False, False)
            tl = TILES - 1
            diag(tl, 1)
            pt_evac(B - 1, 1, B - 2)
            make_wbd(tl, 1, True)
            normed(tl, 1, True)
            residual(tl, 1, 16 * (TILES // 2))
            result(tl, 1, 16 * (TILES // 2 - 1))

        @block.tensor
        def _(pe):
            mm = nc.tensor.matmul
            pe.wait_ge(small_rdy, 1)
            mm(bank[6][:, 0:3 * TILES], sel4_sb[:, :], small[:, :, :].rearrange("q a i -> q (a i)"),
               start=True, stop=True).then_inc(small_ps, 1)
            pe.wait_ge(w_in, 80)

            def project(w, grp_cnt, k, xt_count, free):
                pe.wait_ge(xt_in[k], xt_count)
                if free is not None:
                    pe.wait_ge(nrm_done, free)
                for h in range(2):
                    for t2 in range(2):
                        for c_ in range(2):
                            ins = mm(bank[2 * k + h][:, t2 * 2 * GH:(t2 + 1) * 2 * GH],
                                     xt[:, k, c_, (2 * h + t2) * P:(2 * h + t2 + 1) * P], w[:, c_, :],
                                     start=(c_ == 0), stop=(c_ == 1))
                    ins.then_inc(proj_done, 1)

            for grp in range(NGRP):
                if grp >= 2:
                    pe.wait_ge(vcopy, 2 * (grp - 1))
                project(wkv, grp, grp % 2, 16 * (grp // 2 + 1), grp - 1 if grp >= 2 else None)
                if grp == 0:
                    pe.wait_ge(rows_rdy, 1)
                    for s_ in range(2):
                        ins = nc.tensor.transpose(bank[7][0:NR, s_ * B:(s_ + 1) * B], rows[:, s_, :], ident)
                    ins.then_inc(rows_ps, 1)
            pe.wait_ge(dst_in, 16)
            nc.tensor.transpose(bank[6][:, 128:128 + TILES], dst_it[:, :], ident[0:TILES, 0:TILES]).then_inc(dst_ps, 1)

            def q_transposes(grp, k):
                pe.wait_ge(rope_done, NGRP + grp + 1)
                for h in range(2):
                    if grp >= 1:
                        pe.wait_ge(qt_done, 2 * grp - 1 + h)
                    for t2 in range(2):
                        for m in range(M):
                            ins = nc.tensor.transpose(bank[4 + h][:, (t2 * M + m) * P:(t2 * M + m + 1) * P],
                                                      qr[:, k, 2 * h + t2, m, :], ident)
                    ins.then_inc(qt_ps, 1)

            for grp in range(NGRP):
                if grp < 2:
                    pe.wait_ge(vcopy, 2 * (NGRP - 1 + grp))
                project(wq, NGRP + grp, grp % 2, 16 * (NGRP // 2 + grp // 2 + 1), NGRP + grp - 1)
                if grp >= 1:
                    q_transposes(grp - 1, (grp - 1) % 2)
            q_transposes(NGRP - 1, (NGRP - 1) % 2)

            def keys_t(slots, m, landed, free):
                if free is not None:
                    pe.wait_ge(kt_done, free)
                for i, s in enumerate(slots):
                    pe.wait_ge(win_in[s], landed)
                    for e in range(PAIR):
                        ins = nc.tensor.transpose(bank[4][:, (i * PAIR + e) * P:(i * PAIR + e + 1) * P],
                                                  kv[s][:, e, 0, :], ident)
                ins.then_inc(kt_ps, 1)

            def scores(j, n, tile, free):
                pe.wait_ge(kt_done, n_pair(n, j))
                pe.wait_ge(qbd_done, tile + 1)
                if free is not None:
                    pe.wait_ge(sm_done, free)
                for m in range(M):
                    ins = mm(bank[j % 2][:, m * WIN:(m + 1) * WIN], qbd[(j // 4) % 2][:, j % 4, m, :],
                             kT[(j // 2) % 2][:, j % 2, :], start=True, stop=True)
                ins.then_inc(s_done, 1)

            def n_pair(n, j):
                return n_pairs[0] + (j // 2 + 1)

            n_pairs = [0]

            def pv(j, free):
                k = j % 2
                if free is not None:
                    pe.wait_ge(on_done, free)
                for e in range(PAIR):
                    for g in range(G):
                        ins = mm(bank[5][g * HD:(g + 1) * HD, (j % 4) * 64:(j % 4) * 64 + 64],
                                 kv[j][:, e, 1, g * HD:(g + 1) * HD], pT[k][:, e, :, g * T:(g + 1) * T],
                                 start=(e == 0), stop=(e == PAIR - 1))
                ins.then_inc(pv_done, 1)

            def recips(tile, free):
                pe.wait_ge(rdiag_done, tile + 1)
                if free:
                    pe.wait_ge(on_done, tile)
                mm(bank[5][:, 256:512], c("blk1"), rdiag[:, :, :].rearrange("p a t -> p (a t)"),
                   start=True, stop=True).then_inc(r_done, 1)

            def out_proj(tile, free):
                pe.wait_ge(on_done, tile + 1)
                if free:
                    pe.wait_ge(x1_done, tile)
                for m in range(M):
                    ins = mm(bank[6][:, 0:D], oT[:, m, :, :].rearrange("p b t -> p (b t)"), wo[:, m, :],
                             start=(m == 0), stop=(m == M - 1))
                ins.then_inc(wo_done, 1)

            def subject(tile, k, free):
                pe.wait_ge(x1_done, tile + 1)
                pe.wait_ge(wbd_done, tile + 1)
                if free:
                    pe.wait_ge(ob_done, tile)
                mm(bank[7][:, 0:D], wbd[k][:, :, :].rearrange("p a b -> p (a b)"), x1[k][:, :],
                   start=True, stop=True).then_inc(l1_done, 1)

            pe.wait_ge(qt_done, NB1)
            pe.wait_ge(zeroed, 5)
            keys_t((0, 1), 0, 16, None)
            n_pairs[0] = 0
            scores(0, 0, 0, None)

            def step(it, first, last_):
                for j in range(8):
                    n = it * 8 + j
                    if j % 2 == 0 and not (last_ and j == 6):
                        m = it * 4 + (j // 2 + 1)
                        nx = 16 * (it + 1) if j < 6 else 16 * (it + 2)
                        keys_t(((j + 2) % 8, (j + 3) % 8), m, nx, m)
                    if not (last_ and j == 7):
                        n_pairs[0] = it * 4 if j < 7 else it * 4 + 4
                        scores((j + 1) % 8, n + 1, it * 2 + (j + 1) // 4, None if first and j < 1 else n)
                    pe.wait_ge(exp_done, n + 1)
                    if not (first and j < 2):
                        pe.wait_ge(pt_done, n - 1)
                    for e in range(PAIR):
                        for m in range(M):
                            ins = nc.tensor.transpose(bank[2 + j % 2][0:NR, (e * M + m) * P:(e * M + m + 1) * P],
                                                      pr[j % 2][:, m, e * NR:(e + 1) * NR], ident)
                    ins.then_inc(pt_ps, 1)
                    tl = it * 2 + (j // 4 - 1)
                    tk = (j // 4 + 1) % 2
                    tail = not (first and j < 4)
                    if tail and j % 4 == 0:
                        recips(tl, not (first and j == 4))
                    if not (first and j == 0):
                        pe.wait_ge(pt_done, n)
                        pv((j - 1) % 8, tl + 1 if tail and j % 4 == 1 else None)
                    if tail and j % 4 == 1:
                        out_proj(tl, not (first and j == 5))
                    if tail and j % 4 == 2:
                        subject(tl, tk, not (first and j == 6))

            runs(step)(pe)
            tl = TILES - 1
            recips(tl, True)
            pe.wait_ge(pt_done, B)
            pv(7, None)
            out_proj(tl, True)
            subject(tl, 1, True)


def host_constants():
    import numpy as np
    v = {}
    p = np.arange(P)
    v["iota"] = np.tile(np.arange(NBLK), (P, 1))
    v["upos"] = np.tile((np.arange(PAIR)[:, None] + PAIR * np.arange(NR)[None, :]).ravel(), (P, 1))
    freq = np.float32(1) / np.power(np.float32(10000), np.arange(HALF, dtype=np.float32) / np.float32(HALF))
    v["inv"] = np.tile(freq, (P, 1))
    v["jwin"] = np.tile(np.arange(JW) - WINDOW // BLOCK, (P, 1))
    v["tcol"] = (p % T)[:, None]
    v["own"] = 2 * p[:, None] + np.arange(1, 3)[None, :]
    v["oprow"] = np.tile(np.arange(RB), (P, 1))
    v["eps"] = np.full((P, 1), EPS)
    v["ident"] = np.eye(P)
    v["dmask"] = (p % T)[:, None] == np.arange(T)[None, :]
    v["blk1"] = (p // T)[:, None] == (p // HD)[None, :]
    v["bdm"] = (p // T)[:, None] == np.arange(BT)[None, :]
    v["idxrow"] = np.tile(np.arange(1, NW * B + 1), (P, 1))
    consts = np.concatenate([np.asarray(v[n], np.float32) for n, _ in CONST_COLS], axis=1)
    sel4 = (np.arange(BT)[:, None] == (p // T)[None, :]).astype(np.float32)
    return np.ascontiguousarray(consts), sel4


def kernel(x, itok_Bx257_0_4111, itok_B_37_3939, itok_B_0_7, fside_8xS_0, L0_cond_Wq, L0_cond_Wk, L0_cond_Wv,
           L0_cond_Wo, L0_cond_q_norm_scale, L0_cond_k_norm_scale, L0_cond_k_blocks, L0_cond_v_blocks,
           L1_cond_weights):
    import numpy as np
    import concourse.bacc as bacc
    from concourse.bass_utils import run_bass_kernel_spmd as run

    a = np.asarray
    xf = a(x).reshape(B * T, D)
    kb = a(L0_cond_k_blocks).transpose(0, 2, 1, 3).reshape(CBLK, BLOCK, GH)
    vb = a(L0_cond_v_blocks).transpose(0, 2, 1, 3).reshape(CBLK, BLOCK, GH)
    cache = np.concatenate([kb, vb], axis=2).reshape(CBLK * BLOCK, ROW)
    wq = a(L0_cond_Wq).reshape(G, M, HD, D).transpose(1, 0, 2, 3).reshape(M * GH, D).T
    wkv = np.concatenate([a(L0_cond_Wk), a(L0_cond_Wv)], axis=0).T
    wo = a(L0_cond_Wo).reshape(D, G, M, HD).transpose(2, 1, 3, 0).reshape(M * GH, D)
    wsub = np.concatenate([a(L1_cond_weights).reshape(NSUB * HD, HD), a(fside_8xS_0).reshape(NSUB * HD, 1)], axis=1)
    consts, sel4 = host_constants()
    ins = {
        "xT": xf.T, "x": xf, "table": a(itok_Bx257_0_4111), "p0": a(itok_B_37_3939),
        "p0T": a(itok_B_37_3939).reshape(TILES, BT).T, "subjT": a(itok_B_0_7).reshape(TILES, BT).T,
        "wkvT": wkv, "wqT": wq, "woT": wo, "qs": a(L0_cond_q_norm_scale), "ks": a(L0_cond_k_norm_scale),
        "cache": cache, "wsub": wsub, "consts": consts, "sel4": sel4,
    }
    nc = bacc.Bacc("TRN2", target_bir_lowering=False, num_devices=1)
    arrays, args = {}, []
    for name, v in ins.items():
        v = np.ascontiguousarray(v)
        arrays[f"in_{name}"] = v
        args.append(nc.dram_tensor(f"in_{name}", v.shape, mybir.dt.from_np(v.dtype), kind="ExternalInput").ap())
    out = nc.dram_tensor("out", (B * T, D), F32, kind="ExternalOutput").ap()
    attention_kernel(nc, *args, out)
    r = run(nc, [arrays], core_ids=[0])
    return r.results[0]["out"].reshape(B, T, D)
```

```python
from contextlib import ExitStack

import concourse.bass as bass
from concourse import mybir

ALU = mybir.AluOpType
ACT = mybir.ActivationFunctionType
AX = mybir.AxisListType.X
F32 = mybir.dt.float32
BF16 = mybir.dt.bfloat16
I32 = mybir.dt.int32
I16 = mybir.dt.int16

P = 128
B, T, D = 128, 32, 256
G, M, HD = 4, 2, 32
HALF = HD // 2
GH = G * HD
BLOCK = 16
NBLK = 257
CBLK = 16 * NBLK
WINDOW = 128
TILES = B * T // P
SEEN_AT = 7
K_SCATTERS, Q_SCATTERS = 14, 5
BT = P // T
ROW = 2 * GH
PAIR = 2
NR = 80
WIN = PAIR * NR
NSUB = 8
NW = 3
JW = WINDOW // BLOCK + 3
RB = BLOCK // PAIR
RING = 8
LAG = 1
GT = 4
NGRP = TILES // GT
SCALE = float(D) ** -0.5
EPS = 1e-6
BIG = 2.0 ** 100
MISS = 131072.0
MAGIC = 12582912.0
INV2PI = 0.15915494309189535
TWO_PI = (6.28125, 0.00193500518798828125, 3.019915981956753e-07)
HALF_PI = 1.5707963267948966
PI_IN = 3.1415925

CONST_COLS = [("iota", NBLK), ("upos", WIN), ("inv", HALF), ("jwin", JW), ("tcol", 1), ("batch", 1), ("oprow", RB), ("eps", 1),
              ("ident", P), ("dmask", T), ("blk1", P), ("bdm", BT), ("earlier", 5 * P)]
CO = {}
NCONST = 0
for _name, _w in CONST_COLS:
    CO[_name] = (NCONST, NCONST + _w)
    NCONST += _w


def attention_kernel(nc, xT, x, table, p0, p0T, subj, wkvT, wqT, woT, qs, ks, cache, wsub, consts, sel4, out):
    blk_dram = nc.dram_tensor("block_scratch", [B, JW], F32, kind="Internal").ap()
    ws_dram = nc.dram_tensor("subject_scratch", [B, HD * (HD + 1)], F32, kind="Internal").ap()
    merged = nc.dram_tensor("merged_blocks", [B * NW * BLOCK, ROW], F32, kind="Internal").ap()
    mask_dram = nc.dram_tensor("mask_scratch", [TILES, T, BT, WIN], BF16, kind="Internal").ap()

    with ExitStack() as ctx:
        def sb(name, shape, dt=F32):
            return ctx.enter_context(nc.sbuf_tensor(name, shape, dt))

        def sem(name):
            return ctx.enter_context(nc.semaphore(name))

        bank = [ctx.enter_context(nc.psum_tensor(f"bank{i}", [P, 512], F32)) for i in range(8)]

        cst = sb("cst", [P, NCONST])
        sel4_sb = sb("sel4_sb", [BT, P])
        wkv = sb("wkv", [P, 2, 2 * GH])
        wq = sb("wq", [P, 2, 2 * GH])
        wo = sb("wo", [P, M, D])
        qs_sb = sb("qs_sb", [P, HD])
        ks_sb = sb("ks_sb", [P, HD])
        tab_i = sb("tab_i", [P, NBLK], I32)
        tab = sb("tab", [P, NBLK])
        p0_i = sb("p0_i", [P, 3], I32)
        pra = sb("pra", [P, 3])
        slot = sb("slot", [P, JW])
        blkw = sb("blkw", [P, JW])
        junk = sb("junk", [P, NBLK])
        blk_i = sb("blk_i", [P, NW], I32)
        kvn = sb("kvn", [P, TILES, ROW])
        qr = sb("qr", [P, 2, GT, M, GH])
        qr_flat = qr[:, :, :, :, :].rearrange("p k t m q -> p (k t m q)")
        wrow = qr_flat[:, 0:B * JW].rearrange("p (b j) -> p b j", b=B)
        same = qr_flat[:, B * JW:B * JW + NW * NW * B // 2].bitcast(BF16).rearrange("p (v w b) -> p v w b", v=NW, w=NW)
        seen = kvn[:, SEEN_AT:TILES // 2, :].rearrange("p i c -> p (i c)")[:, 0:NW * JW * B // 2].bitcast(BF16)\
            .rearrange("p (w j b) -> p w j b", w=NW, j=JW)
        rows88 = sb("rows88", [P, 2, JW * RB])
        rows = sb("rows", [P, 2, NR])
        final = sb("final", [P, NW])
        names = sb("names", [P, NW, 3], BF16)
        found = sb("found", [P, JW, 3])
        ge = sb("ge", [P, BLOCK])
        cover = sb("cover", [P, NW, BLOCK + 1], BF16)
        lost = sb("lost", [P, NW, BLOCK + 1])
        entry = sb("entry", [P, JW])
        first_row = sb("first_row", [P, 2, JW])
        sel9 = sb("sel9", [P, RB + 1])
        gidx = sb("gidx", [NR, 2, B], I32)
        gcur = [sb(f"gcur{i}", [NR, 2, BT], I32) for i in range(2)]
        dabs = sb("dabs", [P, NW, BLOCK])
        sel16 = sb("sel16", [P, BLOCK])
        dst_bt = sb("dst_bt", [P, T])
        sidx = sb("sidx", [P, TILES], I32)
        subj_i = sb("subj_i", [P, 1], I32)
        small_i = sb("small_i", [BT, 2, TILES], I32)
        small = sb("small", [BT, 2, TILES])
        pos = sb("pos", [P, TILES])
        par = sb("par", [P, TILES])
        hi = sb("hi", [P, TILES])
        lo = sb("lo", [P, TILES])
        nlo = sb("nlo", [P, TILES])
        nlo2 = sb("nlo2", [P, TILES])
        mrow = sb("mrow", [P, TILES, PAIR, NR], BF16)
        trig = sb("trig", [P, 5, TILES, HALF])
        ang, kk, red, sn, cs = (trig[:, i, :, :] for i in range(5))
        minus_sn = ang
        ccss = {w: (sb(f"cc_{w}", [P, TILES, HD]), sb(f"ss_{w}", [P, TILES, HD])) for w in "kq"}
        mask = [sb(f"mask{i}", [P, BT, WIN], BF16) for i in range(2)]
        wsg = sb("wsg", [P, TILES, HD + 1])
        sq = sb("sq", [P, 2, GT * 2 * GH])
        ra = sb("ra", [P, 2, GT * 2 * GH])
        ssum = sb("ssum", [P, 2, GT * 8])
        rms = sb("rms", [P, 2, GT * 8])
        rin = sb("rin", [P, 2, GT * 8])
        nrm_rb = sb("nrm_rb", [P, 2, 2, GT * 2 * GH])
        nrm, rb = nrm_rb[:, 0, :, :], nrm_rb[:, 1, :, :]
        wall = ra[:, :, :].rearrange("p k n -> p (k n)")[:, 0:HD * (HD + 1)]
        qT = sb("qT", [P, TILES, M, P])
        kv_all = sb("kv_all", [P, RING, PAIR, 2, GH])
        kv = [kv_all[:, i, :, :, :] for i in range(RING)]
        blk_st = [nrm_rb[:, :, :, :].rearrange("p a k n -> p (a k n)"),
                  kv_all[:, :, :, :, :].rearrange("p r a b c -> p (r a b c)")]
        qbd = [sb(f"qbd{i}", [P, BT, M, P]) for i in range(2)]
        tflat = trig[:, :, :, :].rearrange("p a t d -> p (a t d)")
        kT, sm, pr = ([tflat[:, (2 * a + i) * 2 * WIN:(2 * a + i + 1) * 2 * WIN].rearrange("p (m w) -> p m w", m=2)
                       for i in range(2)] for a in range(3))
        nmax = [sb(f"nmax{i}", [P, M]) for i in range(2)]
        pT = [sb(f"pT{i}", [P, PAIR, M, P]) for i in range(2)]
        rsum = [sb(f"rsum{i}", [P, BT * M]) for i in range(2)]
        rinv = sb("rinv", [P, BT * M])
        rdiag = rb[:, 0, 0:256].rearrange("p (a t) -> p a t", t=T)
        oT = rb[:, 0, 256:512].rearrange("p (m b t) -> p m b t", m=M, b=BT)
        rbc = rb[:, 0, 512:768].rearrange("p (a t) -> p a t", t=T)
        xin = [a[:, 0:D] for a in (tab, junk)]
        x1 = [nrm[:, i, 0:D] for i in range(2)]
        ob = [nrm[:, i, D:2 * D] for i in range(2)]
        wbd = [sb(f"wbd{i}", [P, BT, HD]) for i in range(2)]

        def c(name):
            return cst[:, CO[name][0]:CO[name][1]]

        ident = c("ident")

        cst_in = sem("cst_in")
        idx_in = sem("idx_in")
        small_in = sem("small_in")
        w_in = sem("w_in")
        blk_rdy = sem("blk_rdy")
        blk_stored = sem("blk_stored")
        wrow_in = sem("wrow_in")
        blk_in = [sem(f"blk_in{i}") for i in range(2)]
        blk_out = [sem(f"blk_out{w}") for w in range(NW)]
        subj_in = sem("subj_in")
        ws_got = sem("ws_got")
        ws_stored = sem("ws_stored")
        mask_out = sem("mask_out")
        mask_in = [sem(f"mask_in{i}") for i in range(2)]
        xt_in = [sem(f"xt_in{i}") for i in range(NGRP)]
        chain = sem("chain")
        small_rdy = sem("small_rdy")
        small_ps = sem("small_ps")
        rows_rdy = sem("rows_rdy")
        rows_ps = sem("rows_ps")
        gidx_rdy = sem("gidx_rdy")
        same_rdy = sem("same_rdy")
        lost_ps = sem("lost_ps")
        names_rdy = sem("names_rdy")
        seen_rdy = sem("seen_rdy")
        found_ps = sem("found_ps")
        dst_rdy = sem("dst_rdy")
        dst_ps = sem("dst_ps")
        sidx_rdy = sem("sidx_rdy")
        bounds_rdy = sem("bounds_rdy")
        mrow_rdy = sem("mrow_rdy")
        ws_in = sem("ws_in")
        scales_rdy = sem("scales_rdy")
        ang_rdy = sem("ang_rdy")
        sin_done = sem("sin_done")
        rope_rdy = sem("rope_rdy")
        zeroed = sem("zeroed")
        proj_done = sem("proj_done")
        sq_done = sem("sq_done")
        ss_done = sem("ss_done")
        rms_done = sem("rms_done")
        rin_done = sem("rin_done")
        nrm_done = sem("nrm_done")
        vcopy = sem("vcopy")
        ra_done = sem("ra_done")
        rb_done = sem("rb_done")
        rope_done = sem("rope_done")
        qt_ps = sem("qt_ps")
        qt_done = sem("qt_done")
        scat = sem("scat")
        old_in = [sem(f"old_in{i}") for i in range(RING)]
        win_in = [sem(f"win_in{i}") for i in range(RING)]
        gcur_done = sem("gcur_done")
        pool_passed = sem("pool_passed")
        dve_passed = sem("dve_passed")
        kt_ps = sem("kt_ps")
        kt_done = sem("kt_done")
        s_done = sem("s_done")
        sm_done = sem("sm_done")
        exp_done = sem("exp_done")
        pt_ps = sem("pt_ps")
        pt_done = sem("pt_done")
        pv_done = sem("pv_done")
        rinv_done = sem("rinv_done")
        rdiag_done = sem("rdiag_done")
        r_done = sem("r_done")
        rbc_done = sem("rbc_done")
        on_done = sem("on_done")
        wo_done = sem("wo_done")
        x1_done = sem("x1_done")
        l1_done = sem("l1_done")
        ob_done = sem("ob_done")
        qbd_done = sem("qbd_done")
        wbd_done = sem("wbd_done")
        x_in = [sem(f"x_in{i}") for i in range(2)]
        o_out = [sem(f"o_out{i}") for i in range(2)]

        block = ctx.enter_context(nc.Block())
        NB1 = 2 * NGRP
        proj_bank = [(bank[a], bank[a + 1]) for a in (0, 2, 6)]

        def alone(eng, sem_):
            eng.sem_inc(sem_, 1)

        def sizes(cnt):
            heads = G if cnt < NGRP else 2 * G
            return cnt % 2, "k" if cnt < NGRP else "q", heads, GT * heads * HD, cnt % NGRP

        def rope_a(eng, cnt):
            k, w, heads, n, grp = sizes(cnt)
            eng.wait_ge(nrm_done, cnt + 1)
            if cnt >= 2:
                eng.wait_ge(rope_done, cnt - 1)
            a = nrm[:, k, 0:n].rearrange("p (t h d) -> p t h d", t=GT, h=heads)
            cc = ccss[w][0][:, grp * GT:(grp + 1) * GT, :].rearrange("p t (o d) -> p t o d", o=1)\
                .broadcast_to([P, GT, heads, HD])
            eng.tensor_tensor(ra[:, k, 0:n].rearrange("p (t h d) -> p t h d", t=GT, h=heads), a, cc, ALU.mult)\
                .then_inc(ra_done, 1)

        def runs(emit):
            def driver(eng):
                emit(0, True, False)
                with eng.Fori(1, B // 8 - 1) as it:
                    emit(it, False, False)
                emit(B // 8 - 1, False, True)
            return driver

        @block.sync
        def _(sp):
            sp.dma_start(tab_i[:, :], table).then_inc(idx_in, 16)
            sp.dma_start(p0_i[:, 0:1], p0.rearrange("(b o) -> b o", o=1)).then_inc(idx_in, 16)
            sp.dma_start(subj_i[:, :], subj.rearrange("(b o) -> b o", o=1)).then_inc(subj_in, 16)
            sp.dma_start(cst[:, :], consts).then_inc(cst_in, 16)

            def load_xt(grp):
                sp.dma_start(qT[:, grp * GT:(grp + 1) * GT, :, :], xT[:, grp * GT:(grp + 1) * GT, :, :]).then_inc(xt_in[grp], 16)

            load_xt(0)
            load_xt(1)
            sp.wait_ge(blk_rdy, 1)
            sp.dma_start(blk_dram, blkw[:, :]).then_inc(blk_stored, 16)
            sp.wait_ge(blk_stored, 16)
            sp.dma_start(wrow[:, :, :].rearrange("p b j -> p (b j)"),
                         blk_dram.rearrange("b j -> (b j)").partition_broadcast(P)).then_inc(wrow_in, 16)
            for grp in range(2, 6):
                load_xt(grp)
            sp.wait_ge(ws_got, 16)
            sp.dma_start(ws_dram, wall).then_inc(ws_stored, 16)
            sp.wait_ge(ws_stored, 16)
            for q in range(BT):
                sp.dma_start(wsg[q * HD:(q + 1) * HD, :, :],
                             ws_dram.rearrange("(i q) (c e) -> q c i e", q=BT, c=HD)[q]).then_inc(ws_in, 16)
            sp.wait_ge(blk_out[0], 16)
            for grp in range(6, NGRP):
                load_xt(grp)
            sp.wait_ge(mask_out, 16 * BT)

            def load_mask(tile, k):
                for g in range(G):
                    sp.dma_start(mask[k][g * T:(g + 1) * T, :, :].rearrange("t q w -> t (q w)"),
                                 mask_dram[bass.ds(tile, 1), :, :, :].rearrange("i t q w -> (i t) (q w)"))\
                        .then_inc(mask_in[k], 16)

            def load_x(tile, k):
                sp.dma_start(xin[k][:, :], x[bass.ts(tile, P), :]).then_inc(x_in[k], 16)

            def step(it, first, last_):
                for k in range(2):
                    tile = it * 2 + k
                    if not last_:
                        sp.wait_ge(sm_done, tile * 4 + 4)
                        load_mask(tile + 2, k)
                        sp.wait_ge(x1_done, tile + 1)
                        load_x(tile + 2, k)
                    sp.wait_ge(ob_done, tile + 1)
                    sp.dma_start(out[bass.ts(tile, P), :], ob[k][:, :]).then_inc(o_out[k], 16)

            for k in range(2):
                load_mask(k, k)
                load_x(k, k)
            runs(step)(sp)
            for k in range(2):
                sp.wait_ge(o_out[k], 16 * (TILES // 2))

        @block.gpsimd
        def _(pool):
            pool.wait_ge(subj_in, 16)
            pool.indirect_dma_start(wall, None, wsub, bass.IndirectOffsetOnAxis(ap=subj_i[:, :], axis=0),
                                    bounds_check=NSUB - 1, oob_is_err=False).then_inc(ws_got, 16)
            for i in range(2):
                pool.memset(qbd[i][:, :, :, :], 0.0).then_inc(zeroed, 1)
                pool.wait_ge(zeroed, 2 * i + 1)
                pool.memset(pT[i][64:P, :, :, :], 0.0).then_inc(zeroed, 1)
                pool.wait_ge(zeroed, 2 * i + 2)
            def fetch_blocks(i, w):
                pool.indirect_dma_start(blk_st[i], None, cache.rearrange("(r a) c -> r (a c)", a=BLOCK),
                                        bass.IndirectOffsetOnAxis(ap=blk_i[:, w:w + 1], axis=0),
                                        bounds_check=CBLK - 1, oob_is_err=False).then_inc(blk_in[i], 16)

            def store_blocks(i, w):
                pool.wait_ge(blk_in[i], 16)
                pool.dma_start(merged.rearrange("(b w o) c -> b w (o c)", w=NW, o=BLOCK)[:, w, :], blk_st[i])\
                    .then_inc(blk_out[w], 16)

            pool.wait_ge(blk_rdy, 1)
            fetch_blocks(0, 0)
            pool.wait_ge(wrow_in, 16)
            store_blocks(0, 0)
            fetch_blocks(1, 2)

            def tables(w, sc_):
                cc, ss = ccss[w]
                lo_b, hi_b = (sc_[:, h * HALF:(h + 1) * HALF].rearrange("p (o d) -> p o d", o=1)
                              .broadcast_to([P, TILES, HALF]) for h in range(2))
                pool.tensor_tensor(cc[:, :, 0:HALF], cs[:, :, :], lo_b, ALU.mult)
                pool.tensor_tensor(cc[:, :, HALF:HD], cs[:, :, :], hi_b, ALU.mult)
                pool.tensor_tensor(ss[:, :, 0:HALF], minus_sn[:, :, :], hi_b, ALU.mult)
                pool.tensor_tensor(ss[:, :, HALF:HD], sn[:, :, :], lo_b, ALU.mult).then_inc(rope_rdy, 1)

            pool.wait_ge(scales_rdy, 1)
            pool.wait_ge(sin_done, 3)
            tables("k", ks_sb)
            store_blocks(1, 2)
            store_blocks(1, 1)
            tables("q", qs_sb)

            def scatter(i):
                if i % GT == 0:
                    pool.wait_ge(rope_done, i // GT + 1)
                    pool.wait_ge(vcopy, 2 * (i // GT) + 2)
                pool.indirect_dma_start(merged, bass.IndirectOffsetOnAxis(ap=sidx[:, i:i + 1], axis=0), kvn[:, i, :], None,
                                        bounds_check=B * NW * BLOCK - 1, oob_is_err=False).then_inc(scat, 16)

            for w in range(NW):
                pool.wait_ge(blk_out[w], 16)
            pool.wait_ge(sidx_rdy, 1)
            pool.wait_ge(rope_rdy, 2)
            goals = [K_SCATTERS + Q_SCATTERS * grp // 2 for grp in range(NGRP)]
            for grp, start in enumerate([0] + goals[:-1]):
                for i in range(start, min(goals[grp], TILES)):
                    scatter(i)
                rope_a(pool, NGRP + grp)
            for i in range(goals[-1], TILES):
                scatter(i)

            def gather_old(index, k):
                pool.indirect_dma_start(kv[k][0:NR, :, :, :].rearrange("p a b c -> p (a b c)"), None,
                                        cache.rearrange("(r a) c -> r (a c)", a=PAIR),
                                        bass.IndirectOffsetOnAxis(ap=index, axis=0),
                                        bounds_check=CBLK * RB - 1, oob_is_err=False).then_inc(old_in[k], 16)

            def gather_new(index, k):
                pool.indirect_dma_start(kv[k][0:NR, :, :, :].rearrange("p a b c -> p (a b c)"), None,
                                        merged.rearrange("(r a) c -> r (a c)", a=PAIR),
                                        bass.IndirectOffsetOnAxis(ap=index, axis=0),
                                        bounds_check=B * NW * RB - 1, oob_is_err=False).then_inc(win_in[k], 16)

            pool.wait_ge(gidx_rdy, 1)
            pool.wait_ge(zeroed, 8)
            for n in range(4):
                gather_old(gidx[:, 0, n:n + 1], n)
            pool.wait_ge(scat, 16 * TILES)
            for n in range(RING - LAG):
                pool.wait_ge(old_in[n], 16)
                gather_new(gidx[:, 1, n:n + 1], n)
                if n + 4 < RING:
                    gather_old(gidx[:, 0, n + 4:n + 5], n + 4)

            def step(it, first, last_):
                for k in range(2):
                    tile = it * 2 + k
                    if not last_:
                        pool.wait_ge(gcur_done, tile + 1)
                    for j in range(4):
                        if not last_:
                            pool.wait_ge(pv_done, tile * 4 + (j + 1))
                            alone(pool, pool_passed)
                            gather_old(gcur[k][:, 0, j:j + 1], 4 * k + j)
                        if last_ and (k == 1 or j >= LAG):
                            continue
                        kn, jn = (k, j - LAG) if j >= LAG else (1 - k, j + 4 - LAG)
                        pool.wait_ge(old_in[4 * kn + jn], 16 * (it + (1 if kn > k else 2)))
                        alone(pool, pool_passed)
                        gather_new(gidx[:, 1, 4 + jn:5 + jn] if first and kn > k else gcur[kn][:, 1, jn:jn + 1], 4 * kn + jn)

            runs(step)(pool)

        @block.scalar
        def _(act):
            act.dma_start(small_i[:, 0, :], p0T).then_inc(small_in, 16)
            act.dma_start(sel4_sb[:, :], sel4).then_inc(small_in, 16)
            act.dma_start(wkv[:, :, :], wkvT.rearrange("(c p) n -> p c n", p=P)).then_inc(w_in, 16)
            act.dma_start(wq[:, :, :], wqT.rearrange("(c p) n -> p c n", p=P)).then_inc(w_in, 16)
            act.dma_start(wo[:, :, :], woT.rearrange("(m p) n -> p m n", p=P)).then_inc(w_in, 16)
            act.dma_start(qs_sb[:, :], qs.partition_broadcast(P)).then_inc(w_in, 16)
            act.dma_start(ks_sb[:, :], ks.partition_broadcast(P)).then_inc(w_in, 16)

            u2 = c("upos").rearrange("p (e n) -> p e n", e=PAIR)
            NLOW = WINDOW // PAIR

            def masks(tiles):
                for i in tiles:
                    nc.scalar.activation(mrow[:, i, :, 0:NLOW], u2[:, :, 0:NLOW], ACT.Relu, bias=lo[:, i:i + 1], scale=-BIG)
                    nc.scalar.activation(mrow[:, i, :, NLOW:NR], u2[:, :, NLOW:NR], ACT.Relu, bias=hi[:, i:i + 1], scale=BIG)\
                        .then_inc(mrow_rdy, 1)

            def store_masks():
                act.wait_ge(mrow_rdy, TILES)
                for q in range(BT):
                    act.dma_start(mask_dram[:, :, q, :].rearrange("i t w -> t i w"),
                                  mrow[q * T:(q + 1) * T, :, :, :].rearrange("p i e n -> p i (e n)")).then_inc(mask_out, 16)

            act.wait_ge(cst_in, 16)
            act.wait_ge(bounds_rdy, 1)
            masks(range(0, 8))
            act.wait_ge(ang_rdy, 1)
            nc.scalar.activation(sn[:, :, :], red[:, :, :], ACT.Sin).then_inc(sin_done, 1)
            act.wait_ge(ang_rdy, 2)
            nc.scalar.activation(cs[:, :, :], kk[:, :, :], ACT.Sin).then_inc(sin_done, 1)
            nc.scalar.activation(minus_sn[:, :, :], red[:, :, :], ACT.Sin, scale=-1.0).then_inc(sin_done, 1)

            def root(grp_cnt, k, n):
                act.wait_ge(ss_done, grp_cnt + 1)
                nc.scalar.activation(rms[:, k, 0:n], ssum[:, k, 0:n], ACT.Sqrt, bias=c("eps"), scale=1.0 / HD)\
                    .then_inc(rms_done, 1)

            def squares(cnt):
                k = cnt % 2
                for h in range(2):
                    act.wait_ge(proj_done, cnt * 2 + (h + 1))
                    if h == 0 and cnt >= 2:
                        act.wait_ge(ss_done, cnt - 1)
                    ps = proj_bank[cnt % 3][h]
                    src = ps[:, :].rearrange("p (t n) -> p t n", t=2)
                    if cnt == SEEN_AT // GT and h == 0:
                        act.wait_ge(found_ps, 1)
                    if cnt < NGRP:
                        nc.scalar.activation(sq[:, k, h * 2 * GH:(h + 1) * 2 * GH].rearrange("p (t n) -> p t n", t=2),
                                             src[:, :, 0:GH], ACT.Square).then_inc(sq_done, 1)
                        nc.scalar.activation(kvn[:, slice(cnt * GT + 2 * h, cnt * GT + 2 * h + 2), GH:ROW], src[:, :, GH:2 * GH], ACT.Copy)\
                            .then_inc(vcopy, 1)
                    else:
                        nc.scalar.activation(sq[:, k, h * 4 * GH:(h + 1) * 4 * GH], ps[:, :], ACT.Square)\
                            .then_inc(sq_done, 1)

            def evac(grp):
                for h in range(2):
                    act.wait_ge(qt_ps, 2 * grp + h + 1)
                    nc.scalar.activation(qT[:, slice(grp * GT + 2 * h, grp * GT + 2 * h + 2), :, :].rearrange("p t m q -> p (t m q)"),
                                         bank[4 + h][:, :], ACT.Copy).then_inc(qt_done, 1)

            def clear_kv(i):
                act.wait_ge(blk_out[1], 16)
                act.wait_ge(blk_out[2], 16)
                zero = c("iota")[64:P, 0:1].broadcast_to([P - 64, RING // 4 * PAIR * ROW])
                nc.scalar.activation(kv_all[64:P, i * RING // 4:(i + 1) * RING // 4, :, :, :].rearrange("p r a b c -> p (r a b c)"),
                                     zero, ACT.Copy).then_inc(zeroed, 1)

            squares(0)
            squares(1)
            masks(range(8, 14))
            for cnt in range(2 * NGRP):
                if cnt >= 2:
                    squares(cnt)
                if cnt < 6:
                    masks(range(14 + 3 * cnt, 17 + 3 * cnt))
                elif cnt == 6:
                    store_masks()
                if 8 <= cnt < 12:
                    clear_kv(cnt - 8)
                root(cnt, cnt % 2, GT * G if cnt < NGRP else GT * 2 * G)
                if cnt >= NGRP + 3:
                    evac(cnt - NGRP - 3)
            for grp in range(NGRP - 3, NGRP):
                evac(grp)

            def kt_evac(m, k):
                act.wait_ge(kt_ps, m + 1)
                nc.scalar.activation(kT[k][:, :, :].rearrange("p b (e n) -> p (b e) n", e=PAIR),
                                     bank[4][:, :].rearrange("p (b n) -> p b n", b=4)[:, :, 0:NR],
                                     ACT.Copy).then_inc(kt_done, 1)

            def make_qbd(tile, k):
                for g in range(G):
                    ins = nc.scalar.activation(qbd[k][g * HD:(g + 1) * HD, :, :, g * T:(g + 1) * T],
                                               qT[g * HD:(g + 1) * HD, bass.ds(tile, 1), :, :].rearrange(
                                                   "p o m (q t) -> p (o q) m t", q=BT), ACT.Copy, scale=-1.0)
                    if g == G - 1:
                        ins.then_inc(qbd_done, 1)

            act.wait_ge(zeroed, 8)
            act.wait_ge(qt_done, NB1)
            make_qbd(0, 0)
            kt_evac(0, 0)

            def step(it, first, last_):
                for j in range(8):
                    if j % 4 == 1 and not (last_ and j == 5):
                        if not (first and j == 1):
                            act.wait_ge(s_done, it * 8 + (j - 1))
                        make_qbd(it * 2 + (j // 4 + 1), (j // 4 + 1) % 2)
                    n = it * 8 + j
                    b2 = j % 2
                    act.wait_ge(sm_done, n + 1)
                    if not (first and j < 2):
                        act.wait_ge(pt_ps, n - 1)
                    if j % 4 == 0 and not first:
                        act.wait_ge(rinv_done, it * 2 + (j // 4 - 1))
                    for m in range(M):
                        col = (j % 4) * M + m
                        ins = nc.scalar.activation(pr[b2][:, m, :], sm[b2][:, m, :], ACT.Exp,
                                                   bias=nmax[b2][:, m:m + 1], scale=-1.0,
                                                   accum_out=rsum[j // 4][:, col:col + 1])
                    ins.then_inc(exp_done, 1)
                    if j % 2 == 0 and not (last_ and j == 6):
                        if not (first and j == 0):
                            act.wait_ge(s_done, n)
                        kt_evac(it * 4 + (j // 2 + 1), (j // 2 + 1) % 2)

            runs(step)(act)

        @block.vector
        def _(dve):
            n_chain = [0]

            def link(ins):
                n_chain[0] += 1
                ins.then_inc(chain, 1)
                dve.wait_ge(chain, n_chain[0])

            V = nc.vector
            dve.wait_ge(small_in, 32)
            link(V.tensor_scalar(small_i[:, 1, :], small_i[:, 0, :], 1, None, ALU.bitwise_and))
            V.tensor_copy(small[:, :, :], small_i[:, :, :]).then_inc(small_rdy, 1)
            dve.wait_ge(idx_in, 32)
            V.tensor_copy(tab[:, :], tab_i[:, :])
            V.tensor_scalar(p0_i[:, 1:2], p0_i[:, 0:1], 4, None, ALU.arith_shift_right)
            link(V.tensor_scalar(p0_i[:, 2:3], p0_i[:, 0:1], BLOCK - 1, None, ALU.bitwise_and))
            V.tensor_copy(pra[:, 0:1], p0_i[:, 2:3])
            V.tensor_copy(pra[:, 1:2], p0_i[:, 1:2])
            link(V.tensor_scalar(p0_i[:, 0:1], p0_i[:, 2:3], 1, None, ALU.add))
            link(V.tensor_scalar(p0_i[:, 0:1], p0_i[:, 0:1], 1, None, ALU.arith_shift_right))
            V.tensor_copy(pra[:, 2:3], p0_i[:, 0:1])
            dve.wait_ge(cst_in, 16)
            link(V.tensor_scalar(slot[:, :], c("jwin"), pra[:, 1:2], 0.0, ALU.add, ALU.max))
            link(V.tensor_scalar(slot[:, :], slot[:, :], float(NBLK - 1), None, ALU.min))
            for j in range(JW):
                link(V.scalar_tensor_tensor(junk[:, :], c("iota"), slot[:, j:j + 1], tab[:, :], ALU.is_equal, ALU.mult,
                                            accum_out=blkw[:, j:j + 1]))
            V.tensor_copy(blk_i[:, :], blkw[:, JW - NW:JW]).then_inc(blk_rdy, 1)
            dve.wait_ge(small_ps, 1)
            ps = bank[4]
            V.tensor_scalar(pos[:, :], ps[:, 0:TILES], c("tcol"), None, ALU.add)
            link(V.tensor_scalar(par[:, :], ps[:, TILES:2 * TILES], 1.0, None, ALU.mult))
            link(V.scalar_tensor_tensor(nlo[:, :], ps[:, 0:TILES], -128.0, par[:, :], ALU.add, ALU.add))
            V.tensor_scalar(nlo2[:, :], par[:, :], c("tcol"), -1.0, ALU.subtract, ALU.add)
            link(V.tensor_scalar(hi[:, :], par[:, :], -1.0, c("tcol"), ALU.mult, ALU.add))
            V.tensor_scalar(hi[:, :], hi[:, :], 128.0, -BIG, ALU.add, ALU.mult)
            link(V.tensor_tensor(nlo[:, :], nlo[:, :], nlo2[:, :], ALU.min))
            link(V.tensor_scalar(lo[:, :], nlo[:, :], -BIG, None, ALU.mult))
            dve.sem_inc(bounds_rdy, 1)
            pos_b = pos[:, :].rearrange("p (t o) -> p t o", o=1).broadcast_to([P, TILES, HALF])
            inv_b = c("inv").rearrange("p (o d) -> p o d", o=1).broadcast_to([P, TILES, HALF])
            link(V.tensor_tensor(ang[:, :, :], pos_b, inv_b, ALU.mult))

            def reduced(dest, shift):
                link(V.tensor_scalar(kk[:, :, :], ang[:, :, :], INV2PI, shift / (2 * 3.141592653589793), ALU.mult, ALU.add))
                link(V.tensor_scalar(kk[:, :, :], kk[:, :, :], MAGIC, None, ALU.add))
                link(V.tensor_scalar(kk[:, :, :], kk[:, :, :], MAGIC, None, ALU.subtract))
                link(V.scalar_tensor_tensor(dest[:, :, :], kk[:, :, :], -TWO_PI[0], ang[:, :, :], ALU.mult, ALU.add))
                link(V.scalar_tensor_tensor(dest[:, :, :], kk[:, :, :], -TWO_PI[1], dest[:, :, :], ALU.mult, ALU.add))
                link(V.scalar_tensor_tensor(dest[:, :, :], kk[:, :, :], -TWO_PI[2], dest[:, :, :], ALU.mult, ALU.add))

            reduced(red, 0.0)
            link(V.tensor_scalar(red[:, :, :], red[:, :, :], PI_IN, -PI_IN, ALU.min, ALU.max))
            dve.sem_inc(ang_rdy, 1)
            reduced(cs, HALF_PI)
            link(V.tensor_scalar(cs[:, :, :], cs[:, :, :], HALF_PI, PI_IN, ALU.add, ALU.min))
            V.tensor_scalar(kk[:, :, :], cs[:, :, :], -PI_IN, None, ALU.max).then_inc(ang_rdy, 1)

            dve.wait_ge(w_in, 80)
            for sc_ in (qs_sb, ks_sb):
                link(V.tensor_scalar(sc_[:, :], sc_[:, :], 1.0, None, ALU.add))
            dve.sem_inc(scales_rdy, 1)
            V.tensor_scalar(ge[:, :], c("iota")[:, 0:BLOCK], pra[:, 0:1], None, ALU.is_ge)
            V.tensor_scalar(sel16[:, :], c("iota")[:, 0:BLOCK], pra[:, 0:1], None, ALU.is_equal)
            V.tensor_scalar(sel9[:, :], c("iota")[:, 0:RB + 1], pra[:, 2:3], None, ALU.is_equal)
            link(V.memset(cover[:, :, :], 1.0))
            V.tensor_scalar(cover[:, 0, 0:BLOCK], c("iota")[:, 0:BLOCK], pra[:, 0:1], None, ALU.is_ge)
            V.tensor_scalar(cover[:, 2, 0:BLOCK], c("iota")[:, 0:BLOCK], pra[:, 0:1], None, ALU.is_lt)
            dve.wait_ge(wrow_in, 16)
            for w in range(NW):
                ins = V.scalar_tensor_tensor(same[:, w, :, :], wrow[:, :, JW - NW:JW].rearrange("p b j -> p j b"),
                                             blkw[:, JW - NW + w:JW - NW + w + 1],
                                             c("earlier")[:, (2 - w) * P:(5 - w) * P].rearrange("p (j b) -> p j b", j=NW),
                                             ALU.is_equal, ALU.mult)
            ins.then_inc(same_rdy, 1)
            for w in range(NW):
                ins = V.tensor_scalar(seen[:, w, :, :], wrow[:, :, :].rearrange("p b j -> p j b"),
                                      blkw[:, JW - NW + w:JW - NW + w + 1], None, ALU.is_equal)
            ins.then_inc(seen_rdy, 1)
            dve.wait_ge(lost_ps, 1)
            V.tensor_scalar(final[:, :], bank[5][:, 0:NW * (BLOCK + 1)].rearrange("p (w o) -> p w o", w=NW)[:, :, BLOCK], 0.0,
                            None, ALU.is_equal)
            link(V.tensor_scalar(lost[:, :, :].rearrange("p w o -> p (w o)"), bank[5][:, 0:NW * (BLOCK + 1)], 0.0, MISS,
                                 ALU.is_gt, ALU.mult))
            V.tensor_copy(names[:, :, 0], final[:, :])
            V.tensor_scalar(names[:, :, 1], final[:, :], c("batch"), None, ALU.mult)
            link(V.tensor_tensor(names[:, :, 2], final[:, :], c("iota")[:, 0:NW], ALU.mult))
            dve.sem_inc(names_rdy, 1)
            dve.wait_ge(found_ps, 1)
            link(V.tensor_copy(found[:, :, :].rearrange("p j a -> p (j a)"), bank[4][:, 128:128 + 3 * JW]))
            link(V.scalar_tensor_tensor(entry[:, :], found[:, :, 1], float(NW), found[:, :, 2], ALU.mult, ALU.add))
            V.tensor_scalar(first_row[:, 0, 0:NW], entry[:, JW - NW:JW], float(BLOCK), None, ALU.mult)
            link(V.tensor_tensor(dabs[:, :, :], lost[:, :, 0:BLOCK],
                                 c("iota")[:, 0:BLOCK].rearrange("p (w o) -> p w o", w=1).broadcast_to([P, NW, BLOCK]), ALU.add))
            link(V.tensor_tensor(dabs[:, :, :], dabs[:, :, :],
                                 first_row[:, 0, 0:NW].rearrange("p (w o) -> p w o", o=1).broadcast_to([P, NW, BLOCK]), ALU.add))
            da = dabs[:, :, :].rearrange("p w o -> p (w o)")
            link(V.tensor_scalar(dst_bt[:, :], da[:, 0:T], sel16[:, 0:1], None, ALU.mult))
            for v in range(1, BLOCK):
                ins = V.scalar_tensor_tensor(dst_bt[:, :], da[:, v:v + T], sel16[:, v:v + 1], dst_bt[:, :], ALU.mult, ALU.add)
                if v < BLOCK - 1:
                    link(ins)
            ins.then_inc(dst_rdy, 1)
            def gather_rows():
                V.tensor_scalar(first_row[:, 0, :], found[:, :, 0], MISS, None, ALU.mult)
                link(V.tensor_scalar(first_row[:, 1, :], found[:, :, 0], -MISS, MISS, ALU.mult, ALU.add))
                for s_, at in enumerate((blkw, entry)):
                    ins = V.scalar_tensor_tensor(first_row[:, s_, :], at[:, :], float(RB), first_row[:, s_, :], ALU.mult, ALU.add)
                link(ins)
                o_b = c("oprow").rearrange("p (o r) -> p o r", o=1).broadcast_to([P, JW, RB])
                for s_ in range(2):
                    ins = V.tensor_tensor(rows88[:, s_, :].rearrange("p (j o) -> p j o", j=JW),
                                          first_row[:, s_, :].rearrange("p (j o) -> p j o", o=1).broadcast_to([P, JW, RB]),
                                          o_b, ALU.add)
                link(ins)
                link(V.tensor_scalar(rows[:, :, :], rows88[:, :, 0:NR], sel9[:, 0:1], None, ALU.mult))
                for v in range(1, RB + 1):
                    ins = V.scalar_tensor_tensor(rows[:, :, :], rows88[:, :, v:v + NR], sel9[:, v:v + 1], rows[:, :, :],
                                                 ALU.mult, ALU.add)
                    if v < RB:
                        link(ins)
                ins.then_inc(rows_rdy, 1)

            def sums(cnt):
                k, _, heads, n, grp = sizes(cnt)
                dve.wait_ge(sq_done, 2 * cnt + 2)
                V.tensor_reduce(ssum[:, k, 0:GT * heads], sq[:, k, 0:n].rearrange("p (a d) -> p a d", d=HD), AX, ALU.add)\
                    .then_inc(ss_done, 1)

            def invert(cnt):
                k, _, heads, _, _ = sizes(cnt)
                dve.wait_ge(rms_done, cnt + 1)
                V.reciprocal(rin[:, k, 0:GT * heads], rms[:, k, 0:GT * heads]).then_inc(rin_done, 1)

            def norm(cnt):
                k, _, heads, n, grp = sizes(cnt)
                dve.wait_ge(rin_done, cnt + 1)
                for h in range(2):
                    src = proj_bank[cnt % 3][h][:, :].rearrange("p (t a d) -> p t a d", t=2, d=HD)[:, :, 0:heads, :]
                    rv = rin[:, k, h * 2 * heads:(h + 1) * 2 * heads].rearrange("p (t a o) -> p t a o", t=2, o=1)\
                        .broadcast_to([P, 2, heads, HD])
                    ins = V.tensor_tensor(nrm[:, k, h * n // 2:(h + 1) * n // 2].rearrange("p (t a d) -> p t a d", t=2, d=HD),
                                          src, rv, ALU.mult)
                ins.then_inc(nrm_done, 1)

            def rope_b(cnt):
                k, w, heads, n, grp = sizes(cnt)
                if grp == 0:
                    dve.wait_ge(rope_rdy, 1 + cnt // NGRP)
                dve.wait_ge(nrm_done, cnt + 1)
                v4 = nrm[:, k, 0:n].rearrange("p (t a d) -> p t a d", t=GT, d=HD)
                o4 = rb[:, k, 0:n].rearrange("p (t a d) -> p t a d", t=GT, d=HD)
                ss = ccss[w][1][:, grp * GT:(grp + 1) * GT, :].rearrange("p t (o d) -> p t o d", o=1)
                for h in range(2):
                    ins = V.tensor_tensor(o4[:, :, :, h * HALF:(h + 1) * HALF], v4[:, :, :, (1 - h) * HALF:(2 - h) * HALF],
                                          ss[:, :, :, h * HALF:(h + 1) * HALF].broadcast_to([P, GT, heads, HALF]), ALU.mult)
                ins.then_inc(rb_done, 1)

            def roped(cnt):
                k, _, heads, n, grp = sizes(cnt)
                dve.wait_ge(rb_done, cnt + 1)
                dve.wait_ge(ra_done, cnt + 1)
                if cnt < NGRP:
                    dest = kvn[:, grp * GT:(grp + 1) * GT, 0:GH]
                else:
                    if grp >= 2:
                        dve.wait_ge(qt_ps, 2 * grp - 2)
                    dest = qr[:, k, :, :, :].rearrange("p t m q -> p t (m q)")
                V.tensor_tensor(dest, ra[:, k, 0:n].rearrange("p (t n) -> p t n", t=GT),
                                rb[:, k, 0:n].rearrange("p (t n) -> p t n", t=GT), ALU.add).then_inc(rope_done, 1)

            dve.wait_ge(blk_out[0], 16)
            sums(0)
            for cnt in range(2 * NGRP):
                invert(cnt)
                if cnt + 1 < 2 * NGRP:
                    sums(cnt + 1)
                norm(cnt)
                if cnt >= 1:
                    roped(cnt - 1)
                if cnt == 0:
                    dve.wait_ge(ws_stored, 16)
                rope_b(cnt)
                if cnt < NGRP:
                    rope_a(dve, cnt)
                if cnt == 0:
                    dve.wait_ge(dst_ps, 1)
                    V.tensor_copy(sidx[:, :], bank[5][:, 128:128 + TILES]).then_inc(sidx_rdy, 1)
                elif cnt == 4:
                    gather_rows()
                elif cnt == 8:
                    dve.wait_ge(rows_ps, 1)
                    V.tensor_copy(gidx[:, :, :].rearrange("p s b -> p (s b)"), bank[4][0:NR, 0:2 * B]).then_inc(gidx_rdy, 1)
            roped(2 * NGRP - 1)

            def pt_evac(n, k, free):
                dve.wait_ge(pt_ps, n + 1)
                if free is not None:
                    dve.wait_ge(pv_done, free)
                V.tensor_copy(pT[k][0:NR, :, :, :].rearrange("p e m q -> p (e m q)"), bank[2 + k][0:NR, :])\
                    .then_inc(pt_done, 1)

            def diag(tile, k):
                dve.wait_ge(exp_done, tile * 4 + 4)
                V.reciprocal(rinv[:, :], rsum[k][:, :]).then_inc(rinv_done, 1)
                dve.wait_ge(rinv_done, tile + 1)
                V.tensor_tensor(rdiag[:, :, :], c("dmask").rearrange("p (o t) -> p o t", o=1).broadcast_to([P, BT * M, T]),
                                rinv[:, :].rearrange("p (n o) -> p n o", o=1).broadcast_to([P, BT * M, T]), ALU.mult)\
                    .then_inc(rdiag_done, 1)

            def rbc_copy(tile):
                dve.wait_ge(pv_done, tile * 4 + 4)
                dve.wait_ge(r_done, tile + 1)
                V.tensor_copy(rbc[:, :, :].rearrange("p a t -> p (a t)"), bank[5][:, 256:512]).then_inc(rbc_done, 1)

            def normed(tile, k, wait_wo):
                rbc_copy(tile)
                dve.wait_ge(rbc_done, tile + 1)
                if wait_wo:
                    dve.wait_ge(wo_done, tile)
                V.tensor_tensor(oT[:, :, :, :].rearrange("p m b t -> p b m t"),
                                bank[5][:, 0:256].rearrange("p (b m t) -> p b m t", b=BT, m=M),
                                rbc[:, :, :].rearrange("p (b m) t -> p b m t", b=BT), ALU.mult).then_inc(on_done, 1)

            def residual(tile, k, it2):
                dve.wait_ge(wo_done, tile + 1)
                dve.wait_ge(x_in[k], it2)
                V.tensor_tensor(x1[k][:, :], bank[6][:, 0:D], xin[k][:, :], ALU.add).then_inc(x1_done, 1)

            def result(tile, k, stored):
                dve.wait_ge(l1_done, tile + 1)
                if stored is not None:
                    dve.wait_ge(o_out[k], stored)
                V.scalar_tensor_tensor(ob[k][:, :], bank[7][:, 0:D], wsg[:, bass.ds(tile, 1), HD:HD + 1].rearrange("p o d -> p (o d)"),
                                       x1[k][:, :], ALU.add, ALU.add).then_inc(ob_done, 1)

            def step(it, first, last_):
                for j in range(8):
                    n = it * 8 + j
                    b2 = j % 2
                    if j % 4 == 0:
                        dve.wait_ge(mask_in[j // 4], it * 64 + 64)
                    dve.wait_ge(s_done, n + 1)
                    if not (first and j < 2):
                        dve.wait_ge(exp_done, n - 1)
                    alone(dve, dve_passed)
                    for m in range(M):
                        ins = V.tensor_tensor_reduce(out=sm[b2][:, m, :], in0=bank[b2][:, m * WIN:(m + 1) * WIN],
                                                     in1=mask[j // 4][:, j % 4, :],
                                                     scale=SCALE, scalar=3.0e38, op0=ALU.add, op1=ALU.min,
                                                     accum_out=nmax[b2][:, m:m + 1])
                    ins.then_inc(sm_done, 1)
                    if j % 4 == 1 and not last_:
                        V.tensor_copy(gcur[j // 4][:, :, :], gidx[:, :, bass.ds(it * 8 + (4 * (j // 4) + RING), 4)])\
                            .then_inc(gcur_done, 1)
                    tl = it * 2 + (j // 4 - 1)
                    tk = (j // 4 + 1) % 2
                    tail = not (first and j < 4)
                    if j % 4 == 0 and tail:
                        diag(tl, tk)
                    if not (first and j == 0):
                        pt_evac(n - 1, (j - 1) % 2, None if first and j <= 2 else n - 2)
                    if not tail or j % 4 == 0:
                        continue
                    if j % 4 == 1:
                        make_wbd(tl, tk, not (isinstance(it, int) and tl <= 1))
                        normed(tl, tk, not (first and j < 8 and j // 4 == 1))
                    elif j % 4 == 2:
                        residual(tl, tk, 16 * (it + 1) if j > 4 else 16 * it)
                    else:
                        result(tl, tk, None if first else (16 * it if j > 4 else 16 * (it - 1)) if not isinstance(it, int)
                               else max(0, 16 * it if j > 4 else 16 * (it - 1)) or None)

            def make_wbd(tile, k, used):
                if used:
                    dve.wait_ge(l1_done, tile - 1)
                w = wsg[:, bass.ds(tile, 1), 0:HD].broadcast_to([P, BT, HD])
                m = c("bdm").rearrange("p (q o) -> p q o", o=1).broadcast_to([P, BT, HD])
                V.tensor_tensor(wbd[k][:, :, :], w, m, ALU.mult).then_inc(wbd_done, 1)

            dve.wait_ge(zeroed, 8)
            dve.wait_ge(ws_in, 16 * BT)
            step(0, True, False)
            step(1, False, False)
            with dve.Fori(2, B // 8 - 1) as it:
                step(it, False, False)
            step(B // 8 - 1, False, True)
            tl = TILES - 1
            diag(tl, 1)
            pt_evac(B - 1, 1, B - 2)
            make_wbd(tl, 1, True)
            normed(tl, 1, True)
            residual(tl, 1, 16 * (TILES // 2))
            result(tl, 1, 16 * (TILES // 2 - 1))

        @block.tensor
        def _(pe):
            mm = nc.tensor.matmul
            pe.wait_ge(small_rdy, 1)
            mm(bank[4][:, 0:2 * TILES], sel4_sb[:, :], small[:, :, :].rearrange("q a i -> q (a i)"),
               start=True, stop=True).then_inc(small_ps, 1)
            pe.wait_ge(w_in, 80)

            def project(cnt):
                w = wkv if cnt < NGRP else wq
                pe.wait_ge(xt_in[cnt % NGRP], 16)
                if cnt >= 3:
                    pe.wait_ge(nrm_done, cnt - 2)
                    pe.wait_ge(vcopy, 2 * min(cnt - 2, NGRP))
                    pe.wait_ge(sq_done, 2 * (cnt - 2))
                for h in range(2):
                    for t2 in range(2):
                        for c_ in range(2):
                            ins = mm(proj_bank[cnt % 3][h][:, t2 * 2 * GH:(t2 + 1) * 2 * GH],
                                     qT[:, cnt % NGRP * GT + 2 * h + t2, c_, :], w[:, c_, :],
                                     start=(c_ == 0), stop=(c_ == 1))
                    ins.then_inc(proj_done, 1)

            def q_transposes(grp, k):
                pe.wait_ge(rope_done, NGRP + grp + 1)
                for h in range(2):
                    if grp >= 1:
                        pe.wait_ge(qt_done, 2 * grp - 1 + h)
                    for t2 in range(2):
                        for m in range(M):
                            ins = nc.tensor.transpose(bank[4 + h][:, (t2 * M + m) * P:(t2 * M + m + 1) * P],
                                                      qr[:, k, 2 * h + t2, m, :], ident)
                    ins.then_inc(qt_ps, 1)

            for cnt in range(2):
                project(cnt)
            pe.wait_ge(same_rdy, 1)
            for w in range(NW):
                for w2 in range(NW):
                    ins = mm(bank[5][:, w * (BLOCK + 1):(w + 1) * (BLOCK + 1)], same[:, w2, w, :], cover[:, w2, :],
                             start=(w2 == 0), stop=(w2 == NW - 1))
            ins.then_inc(lost_ps, 1)
            pe.wait_ge(names_rdy, 1)
            pe.wait_ge(seen_rdy, 1)
            for j in range(JW):
                for w2 in range(NW):
                    ins = mm(bank[4][:, 128 + 3 * j:131 + 3 * j], seen[:, w2, j, :], names[:, w2, :],
                             start=(w2 == 0), stop=(w2 == NW - 1))
            ins.then_inc(found_ps, 1)
            pe.wait_ge(dst_rdy, 1)
            for q in range(BT):
                ins = mm(bank[5][q * T:(q + 1) * T, 128:128 + TILES], dst_bt[:, :],
                         ident.rearrange("p (i q) -> p q i", q=BT)[:, q, :], start=True, stop=True)
            ins.then_inc(dst_ps, 1)
            for cnt in range(2, 2 * NGRP):
                project(cnt)
                if cnt == NGRP - 1:
                    pe.wait_ge(rows_rdy, 1)
                    for s_ in range(2):
                        ins = nc.tensor.transpose(bank[4][0:NR, s_ * B:(s_ + 1) * B], rows[:, s_, :], ident)
                    ins.then_inc(rows_ps, 1)
                if cnt >= NGRP + 3:
                    q_transposes(cnt - NGRP - 3, (cnt - 3) % 2)
            for grp in range(NGRP - 3, NGRP):
                q_transposes(grp, grp % 2)

            def keys_t(slots, m, landed, free):
                if free is not None:
                    pe.wait_ge(kt_done, free)
                for i, s in enumerate(slots):
                    pe.wait_ge(win_in[s], landed)
                    for e in range(PAIR):
                        ins = nc.tensor.transpose(bank[4][:, (i * PAIR + e) * P:(i * PAIR + e + 1) * P],
                                                  kv[s][:, e, 0, :], ident)
                ins.then_inc(kt_ps, 1)

            def scores(j, n, tile, free):
                pe.wait_ge(kt_done, n_pair(n, j))
                pe.wait_ge(qbd_done, tile + 1)
                if free is not None:
                    pe.wait_ge(sm_done, free)
                for m in range(M):
                    ins = mm(bank[j % 2][:, m * WIN:(m + 1) * WIN], qbd[(j // 4) % 2][:, j % 4, m, :],
                             kT[(j // 2) % 2][:, j % 2, :], start=True, stop=True)
                ins.then_inc(s_done, 1)

            def n_pair(n, j):
                return n_pairs[0] + (j // 2 + 1)

            n_pairs = [0]

            def pv(j, free):
                k = j % 2
                if free is not None:
                    pe.wait_ge(on_done, free)
                for e in range(PAIR):
                    for g in range(G):
                        ins = mm(bank[5][g * HD:(g + 1) * HD, (j % 4) * 64:(j % 4) * 64 + 64],
                                 kv[j][:, e, 1, g * HD:(g + 1) * HD], pT[k][:, e, :, g * T:(g + 1) * T],
                                 start=(e == 0), stop=(e == PAIR - 1))
                ins.then_inc(pv_done, 1)

            def recips(tile, free):
                pe.wait_ge(rdiag_done, tile + 1)
                if free:
                    pe.wait_ge(on_done, tile)
                mm(bank[5][:, 256:512], c("blk1"), rdiag[:, :, :].rearrange("p a t -> p (a t)"),
                   start=True, stop=True).then_inc(r_done, 1)

            def out_proj(tile, free):
                pe.wait_ge(on_done, tile + 1)
                if free:
                    pe.wait_ge(x1_done, tile)
                for m in range(M):
                    ins = mm(bank[6][:, 0:D], oT[:, m, :, :].rearrange("p b t -> p (b t)"), wo[:, m, :],
                             start=(m == 0), stop=(m == M - 1))
                ins.then_inc(wo_done, 1)

            def subject(tile, k, free):
                pe.wait_ge(x1_done, tile + 1)
                pe.wait_ge(wbd_done, tile + 1)
                if free:
                    pe.wait_ge(ob_done, tile)
                mm(bank[7][:, 0:D], wbd[k][:, :, :].rearrange("p a b -> p (a b)"), x1[k][:, :],
                   start=True, stop=True).then_inc(l1_done, 1)

            pe.wait_ge(qt_done, NB1)
            pe.wait_ge(zeroed, 8)
            keys_t((0, 1), 0, 16, None)
            n_pairs[0] = 0
            scores(0, 0, 0, None)

            def step(it, first, last_):
                for j in range(8):
                    n = it * 8 + j
                    if j % 2 == 0 and not (last_ and j == 6):
                        m = it * 4 + (j // 2 + 1)
                        nx = 16 * (it + 1) if j < 6 else 16 * (it + 2)
                        keys_t(((j + 2) % 8, (j + 3) % 8), m, nx, m)
                    if not (last_ and j == 7):
                        n_pairs[0] = it * 4 if j < 7 else it * 4 + 4
                        scores((j + 1) % 8, n + 1, it * 2 + (j + 1) // 4, None if first and j < 1 else n)
                    pe.wait_ge(exp_done, n + 1)
                    if not (first and j < 2):
                        pe.wait_ge(pt_done, n - 1)
                    for e in range(PAIR):
                        for m in range(M):
                            ins = nc.tensor.transpose(bank[2 + j % 2][0:NR, (e * M + m) * P:(e * M + m + 1) * P],
                                                      pr[j % 2][:, m, e * NR:(e + 1) * NR], ident)
                    ins.then_inc(pt_ps, 1)
                    tl = it * 2 + (j // 4 - 1)
                    tk = (j // 4 + 1) % 2
                    tail = not (first and j < 4)
                    if tail and j % 4 == 0:
                        recips(tl, not (first and j == 4))
                    if not (first and j == 0):
                        pe.wait_ge(pt_done, n)
                        pv((j - 1) % 8, tl + 1 if tail and j % 4 == 1 else None)
                    if tail and j % 4 == 1:
                        out_proj(tl, not (first and j == 5))
                    if tail and j % 4 == 2:
                        subject(tl, tk, not (first and j == 6))

            runs(step)(pe)
            tl = TILES - 1
            recips(tl, True)
            pe.wait_ge(pt_done, B)
            pv(7, None)
            out_proj(tl, True)
            subject(tl, 1, True)


def host_constants():
    import numpy as np
    v = {}
    p = np.arange(P)
    v["iota"] = np.tile(np.arange(NBLK), (P, 1))
    v["upos"] = np.tile((np.arange(PAIR)[:, None] + PAIR * np.arange(NR)[None, :]).ravel(), (P, 1))
    freq = np.float32(1) / np.power(np.float32(10000), np.arange(HALF, dtype=np.float32) / np.float32(HALF))
    v["inv"] = np.tile(freq, (P, 1))
    v["jwin"] = np.tile(np.arange(JW) - WINDOW // BLOCK, (P, 1))
    v["tcol"] = (p % T)[:, None]
    v["batch"] = p[:, None]
    v["oprow"] = np.tile(np.arange(RB), (P, 1))
    v["eps"] = np.full((P, 1), EPS)
    v["ident"] = np.eye(P)
    v["dmask"] = (p % T)[:, None] == np.arange(T)[None, :]
    v["blk1"] = (p // T)[:, None] == (p // HD)[None, :]
    v["bdm"] = (p // T)[:, None] == np.arange(BT)[None, :]
    v["earlier"] = np.concatenate([p[None, :] <= p[:, None]] * 2 + [p[None, :] < p[:, None]] * 3, axis=1)
    consts = np.concatenate([np.asarray(v[n], np.float32) for n, _ in CONST_COLS], axis=1)
    sel4 = (np.arange(BT)[:, None] == (p // T)[None, :]).astype(np.float32)
    return np.ascontiguousarray(consts), sel4


def kernel(x, itok_Bx257_0_4111, itok_B_37_3939, itok_B_0_7, fside_8xS_0, L0_cond_Wq, L0_cond_Wk, L0_cond_Wv,
           L0_cond_Wo, L0_cond_q_norm_scale, L0_cond_k_norm_scale, L0_cond_k_blocks, L0_cond_v_blocks,
           L1_cond_weights):
    import numpy as np
    import concourse.bacc as bacc
    from concourse.bass_utils import run_bass_kernel_spmd as run

    a = np.asarray
    xf = a(x).reshape(B * T, D)
    kb = a(L0_cond_k_blocks).transpose(0, 2, 1, 3).reshape(CBLK, BLOCK, GH)
    vb = a(L0_cond_v_blocks).transpose(0, 2, 1, 3).reshape(CBLK, BLOCK, GH)
    cache = np.concatenate([kb, vb], axis=2).reshape(CBLK * BLOCK, ROW)
    wq = a(L0_cond_Wq).reshape(G, M, HD, D).transpose(1, 0, 2, 3).reshape(M * GH, D).T
    wkv = np.concatenate([a(L0_cond_Wk), a(L0_cond_Wv)], axis=0).T
    wo = a(L0_cond_Wo).reshape(D, G, M, HD).transpose(2, 1, 3, 0).reshape(M * GH, D)
    wsub = np.concatenate([a(L1_cond_weights), a(fside_8xS_0)[:, :, None]], axis=2).reshape(NSUB, HD * (HD + 1))
    consts, sel4 = host_constants()
    ins = {
        "xT": xf.reshape(TILES, P, 2, P).transpose(3, 0, 2, 1), "x": xf, "table": a(itok_Bx257_0_4111), "p0": a(itok_B_37_3939),
        "p0T": a(itok_B_37_3939).reshape(TILES, BT).T, "subj": a(itok_B_0_7),
        "wkvT": wkv, "wqT": wq, "woT": wo, "qs": a(L0_cond_q_norm_scale), "ks": a(L0_cond_k_norm_scale),
        "cache": cache, "wsub": wsub, "consts": consts, "sel4": sel4,
    }
    nc = bacc.Bacc("TRN2", target_bir_lowering=False, num_devices=1)
    arrays, args = {}, []
    for name, v in ins.items():
        v = np.ascontiguousarray(v)
        arrays[f"in_{name}"] = v
        args.append(nc.dram_tensor(f"in_{name}", v.shape, mybir.dt.from_np(v.dtype), kind="ExternalInput").ap())
    out = nc.dram_tensor("out", (B * T, D), F32, kind="ExternalOutput").ap()
    attention_kernel(nc, *args, out)
    r = run(nc, [arrays], core_ids=[0])
    return r.results[0]["out"].reshape(B, T, D)
```

```python
from contextlib import ExitStack

import concourse.bass as bass
from concourse import mybir

ALU = mybir.AluOpType
ACT = mybir.ActivationFunctionType
AX = mybir.AxisListType.X
F32 = mybir.dt.float32
BF16 = mybir.dt.bfloat16
I32 = mybir.dt.int32

P = 128
B, T, D = 128, 32, 256
G, M, HD = 4, 2, 32
HALF = HD // 2
GH = G * HD
BLOCK = 16
NBLK = 257
CBLK = 16 * NBLK
WINDOW = 128
TILES = B * T // P
BT = P // T
ROW = 2 * GH
PAIR = 2
NR = 80
WIN = PAIR * NR
NSUB = 8
NW = 3
JW = WINDOW // BLOCK + 3
RB = BLOCK // PAIR
RING = 8
LAG = 1
GT = 4
NGRP = TILES // GT
KT_ROWS = 96
SEEN_AT = 7
EARLY = 6
DVE_ROPE = (7,)
K_SCATTERS, Q_SCATTERS = 14, 5
SCALE = float(D) ** -0.5
EPS = 1e-6
BIG = 2.0 ** 100
MISS = 131072.0
MAGIC = 12582912.0
INV2PI = 0.15915494309189535
TWO_PI = (6.28125, 0.00193500518798828125, 3.019915981956753e-07)
HALF_PI = 1.5707963267948966
PI_IN = 3.1415925

CONST_COLS = [("iota", NBLK), ("upos", WIN), ("inv", HALF), ("jwin", JW), ("tcol", 1), ("batch", 1), ("oprow", RB), ("eps", 1),
              ("ident", P), ("dmask", T), ("blk1", P), ("bdm", BT), ("upto", P), ("before", P)]
CO = {}
NCONST = 0
for _name, _w in CONST_COLS:
    CO[_name] = (NCONST, NCONST + _w)
    NCONST += _w


def attention_kernel(nc, xT, x, table, p0, p0T, subj, wkvT, wqT, woT, qs, ks, cache, wsub, consts, sel4, out):
    blk_dram = nc.dram_tensor("block_scratch", [B, JW], F32, kind="Internal").ap()
    ws_dram = nc.dram_tensor("subject_scratch", [B, HD * (HD + 1)], F32, kind="Internal").ap()
    merged = nc.dram_tensor("merged_blocks", [B * NW * BLOCK, ROW], F32, kind="Internal").ap()
    mask_dram = nc.dram_tensor("mask_scratch", [TILES, T, BT, WIN], BF16, kind="Internal").ap()

    with ExitStack() as ctx:
        def sb(name, shape, dt=F32):
            return ctx.enter_context(nc.sbuf_tensor(name, shape, dt))

        def sem(name):
            return ctx.enter_context(nc.semaphore(name))

        bank = [ctx.enter_context(nc.psum_tensor(f"bank{i}", [P, 512], F32)) for i in range(8)]

        cst = sb("cst", [P, NCONST])
        sel4_sb = sb("sel4_sb", [BT, P])
        wkv = sb("wkv", [P, 2, 2 * GH])
        wq = sb("wq", [P, 2, 2 * GH])
        wo = sb("wo", [P, M, D])
        qs_sb = sb("qs_sb", [P, HD])
        ks_sb = sb("ks_sb", [P, HD])
        tab_i = sb("tab_i", [P, NBLK], I32)
        tab = sb("tab", [P, NBLK])
        p0_i = sb("p0_i", [P, 3], I32)
        pra = sb("pra", [P, 3])
        slot = sb("slot", [P, JW])
        blkw = sb("blkw", [P, JW])
        junk = sb("junk", [P, NBLK])
        blk_i = sb("blk_i", [P, NW], I32)
        kvn = sb("kvn", [P, TILES, ROW])
        qr = sb("qr", [P, 2, GT, M, GH])
        qr_flat = qr[:, :, :, :, :].rearrange("p k t m q -> p (k t m q)")
        wrow = qr_flat[:, 0:B * JW].rearrange("p (b j) -> p b j", b=B)
        same = qr_flat[:, B * JW:B * JW + NW * NW * B // 2].bitcast(BF16).rearrange("p (v w b) -> p v w b", v=NW, w=NW)
        seen = kvn[:, SEEN_AT:TILES // 2, :].rearrange("p i c -> p (i c)")[:, 0:NW * JW * B // 2].bitcast(BF16)\
            .rearrange("p (w j b) -> p w j b", w=NW, j=JW)
        rows88 = sb("rows88", [P, 2, JW * RB])
        rows = sb("rows", [P, 2, NR])
        final = sb("final", [P, NW])
        names = sb("names", [P, NW, 3], BF16)
        found = sb("found", [P, JW, 3])
        ge = sb("ge", [P, BLOCK])
        cover = sb("cover", [P, NW, BLOCK + 1], BF16)
        lost = sb("lost", [P, NW, BLOCK + 1])
        entry = sb("entry", [P, JW])
        first_row = sb("first_row", [P, 2, JW])
        sel9 = sb("sel9", [P, RB + 1])
        gidx = sb("gidx", [NR, 2, B], I32)
        gcur = [sb(f"gcur{i}", [NR, 2, BT], I32) for i in range(2)]
        dabs = sb("dabs", [P, NW, BLOCK])
        sel16 = sb("sel16", [P, BLOCK])
        dst_bt = sb("dst_bt", [P, T])
        sidx = sb("sidx", [P, TILES], I32)
        subj_i = sb("subj_i", [P, 1], I32)
        small_i = sb("small_i", [BT, 2, TILES], I32)
        small = sb("small", [BT, 2, TILES])
        pos = sb("pos", [P, TILES])
        par = sb("par", [P, TILES])
        hi = sb("hi", [P, TILES])
        lo = sb("lo", [P, TILES])
        nlo = sb("nlo", [P, TILES])
        nlo2 = sb("nlo2", [P, TILES])
        mrow = sb("mrow", [P, TILES, PAIR, NR], BF16)
        trig = sb("trig", [P, 5, TILES, HALF])
        ang, kk, red, sn, cs = (trig[:, i, :, :] for i in range(5))
        minus_sn = ang
        ccss = {w: (sb(f"cc_{w}", [P, TILES, HD]), sb(f"ss_{w}", [P, TILES, HD])) for w in "kq"}
        mask = [sb(f"mask{i}", [P, BT, WIN], BF16) for i in range(2)]
        wsg = sb("wsg", [P, TILES, HD + 1])
        sq = sb("sq", [P, 2, GT * 2 * GH])
        ra = sb("ra", [P, 2, GT * 2 * GH])
        ssum = sb("ssum", [P, 2, GT * 8])
        rms = sb("rms", [P, 2, GT * 8])
        rin = sb("rin", [P, 2, GT * 8])
        nrm_rb = sb("nrm_rb", [P, 2, 2, GT * 2 * GH])
        nrm, rb = nrm_rb[:, 0, :, :], nrm_rb[:, 1, :, :]
        wall = wsg[:, :, :].rearrange("p i d -> p (i d)")
        qT = sb("qT", [P, TILES, M, P])
        kv_all = sb("kv_all", [P, RING, PAIR, 2, GH])
        kv = [kv_all[:, i, :, :, :] for i in range(RING)]
        blk_st = [nrm_rb[:, :, :, :].rearrange("p a k n -> p (a k n)"),
                  kvn[:, TILES // 2:TILES, :].rearrange("p i c -> p (i c)")]
        qbd = [sb(f"qbd{i}", [P, BT, M, P]) for i in range(2)]
        tflat = trig[:, :, :, :].rearrange("p a t d -> p (a t d)")
        kT = [tflat[:, i * WIN:(i + 1) * WIN] for i in range(2)]
        sm, pr = ([tflat[:, (2 * a + i) * M * WIN:(2 * a + i + 1) * M * WIN].rearrange("p (m w) -> p m w", m=M)
                   for i in range(2)] for a in range(1, 3))
        nmax = [sb(f"nmax{i}", [P, M]) for i in range(2)]
        pT = [sb(f"pT{i}", [P, PAIR, M, P]) for i in range(2)]
        rsum = [sb(f"rsum{i}", [P, BT * M]) for i in range(2)]
        rinv = sb("rinv", [P, BT * M])
        rdiag = rb[:, 0, 0:256].rearrange("p (a t) -> p a t", t=T)
        oT = rb[:, 0, 256:512].rearrange("p (m b t) -> p m b t", m=M, b=BT)
        rbc = rb[:, 0, 512:768].rearrange("p (a t) -> p a t", t=T)
        xin = [a[:, 0:D] for a in (tab, junk)]
        x1 = [nrm[:, i, 0:D] for i in range(2)]
        ob = [nrm[:, i, D:2 * D] for i in range(2)]
        wbd = [sb(f"wbd{i}", [P, BT, HD]) for i in range(2)]

        def c(name):
            return cst[:, CO[name][0]:CO[name][1]]

        ident = c("ident")

        cst_in = sem("cst_in")
        idx_in = sem("idx_in")
        small_in = sem("small_in")
        w_in = sem("w_in")
        blk_i_rdy = sem("blk_i_rdy")
        blk_rdy = sem("blk_rdy")
        blk_stored = sem("blk_stored")
        wrow_in = sem("wrow_in")
        blk_in = [sem(f"blk_in{i}") for i in range(2)]
        blk_out = [sem(f"blk_out{w}") for w in range(NW)]
        subj_in = sem("subj_in")
        ws_got = sem("ws_got")
        ws_stored = sem("ws_stored")
        mask_out = sem("mask_out")
        mask_in = [sem(f"mask_in{i}") for i in range(2)]
        xt_in = [sem(f"xt_in{i}") for i in range(NGRP)]
        chain = sem("chain")
        small_rdy = sem("small_rdy")
        small_ps = sem("small_ps")
        rows_rdy = sem("rows_rdy")
        rows_ps = sem("rows_ps")
        gidx_rdy = sem("gidx_rdy")
        same_rdy = sem("same_rdy")
        lost_ps = sem("lost_ps")
        names_rdy = sem("names_rdy")
        seen_rdy = sem("seen_rdy")
        found_ps = sem("found_ps")
        dst_rdy = sem("dst_rdy")
        dst_ps = sem("dst_ps")
        sidx_rdy = sem("sidx_rdy")
        bounds_rdy = sem("bounds_rdy")
        mrow_rdy = sem("mrow_rdy")
        ws_in = sem("ws_in")
        scales_rdy = sem("scales_rdy")
        ang_rdy = sem("ang_rdy")
        sin_done = sem("sin_done")
        rope_rdy = sem("rope_rdy")
        zeroed = sem("zeroed")
        proj_done = sem("proj_done")
        sq_done = sem("sq_done")
        ss_done = sem("ss_done")
        rms_done = sem("rms_done")
        rin_done = sem("rin_done")
        nrm_done = sem("nrm_done")
        vcopy = sem("vcopy")
        ra_done = sem("ra_done")
        rb_done = sem("rb_done")
        rope_done = sem("rope_done")
        qt_ps = sem("qt_ps")
        qt_done = sem("qt_done")
        scat = sem("scat")
        old_in = [sem(f"old_in{i}") for i in range(RING)]
        win_in = [sem(f"win_in{i}") for i in range(RING)]
        gcur_done = [sem(f"gcur_done{i}") for i in range(2)]
        pool_passed = sem("pool_passed")
        dve_passed = sem("dve_passed")
        kt_ps = sem("kt_ps")
        kt_done = sem("kt_done")
        s_done = sem("s_done")
        sm_done = sem("sm_done")
        exp_done = sem("exp_done")
        pt_ps = sem("pt_ps")
        pt_done = sem("pt_done")
        pv_done = sem("pv_done")
        rinv_done = sem("rinv_done")
        rdiag_done = sem("rdiag_done")
        r_done = sem("r_done")
        rbc_done = sem("rbc_done")
        on_done = sem("on_done")
        wo_done = sem("wo_done")
        x1_done = sem("x1_done")
        l1_done = sem("l1_done")
        ob_done = sem("ob_done")
        qbd_done = sem("qbd_done")
        wbd_done = sem("wbd_done")
        x_in = [sem(f"x_in{i}") for i in range(2)]
        o_out = [sem(f"o_out{i}") for i in range(2)]

        block = ctx.enter_context(nc.Block())
        NB1 = 2 * NGRP
        proj_bank = [(bank[a], bank[a + 1]) for a in (0, 2, 6)]

        def alone(eng, sem_):
            eng.sem_inc(sem_, 1)

        def sizes(cnt):
            heads = G if cnt < NGRP else 2 * G
            return cnt % 2, "k" if cnt < NGRP else "q", heads, GT * heads * HD, cnt % NGRP

        def rope_a(eng, cnt):
            k, w, heads, n, grp = sizes(cnt)
            eng.wait_ge(nrm_done, cnt + 1)
            if cnt >= 2:
                eng.wait_ge(rope_done, cnt - 1)
            a = nrm[:, k, 0:n].rearrange("p (t h d) -> p t h d", t=GT, h=heads)
            cc = ccss[w][0][:, grp * GT:(grp + 1) * GT, :].rearrange("p t (o d) -> p t o d", o=1)\
                .broadcast_to([P, GT, heads, HD])
            eng.tensor_tensor(ra[:, k, 0:n].rearrange("p (t h d) -> p t h d", t=GT, h=heads), a, cc, ALU.mult)\
                .then_inc(ra_done, 1)

        def runs(emit):
            def driver(eng):
                emit(0, True, False)
                with eng.Fori(1, B // 8 - 1) as it:
                    emit(it, False, False)
                emit(B // 8 - 1, False, True)
            return driver

        @block.sync
        def _(sp):
            sp.dma_start(tab_i[:, :], table).then_inc(idx_in, 16)
            sp.dma_start(p0_i[:, 0:1], p0.rearrange("(b o) -> b o", o=1)).then_inc(idx_in, 16)
            sp.dma_start(subj_i[:, :], subj.rearrange("(b o) -> b o", o=1)).then_inc(subj_in, 16)
            sp.dma_start(cst[:, :], consts).then_inc(cst_in, 16)

            def load_xt(grp):
                sp.dma_start(qT[:, grp * GT:(grp + 1) * GT, :, :], xT[:, grp * GT:(grp + 1) * GT, :, :]).then_inc(xt_in[grp], 16)

            load_xt(0)
            load_xt(1)
            sp.wait_ge(blk_rdy, 1)
            sp.dma_start(blk_dram, blkw[:, :]).then_inc(blk_stored, 16)
            sp.wait_ge(blk_stored, 16)
            sp.dma_start(wrow[:, :, :].rearrange("p b j -> p (b j)"),
                         blk_dram.rearrange("b j -> (b j)").partition_broadcast(P)).then_inc(wrow_in, 16)
            for grp in range(2, 6):
                load_xt(grp)
            sp.wait_ge(blk_out[0], 16)
            for grp in range(6, NGRP):
                load_xt(grp)
            sp.wait_ge(blk_out[1], 64)
            sp.wait_ge(ws_got, 16)
            sp.dma_start(ws_dram, wall).then_inc(ws_stored, 16)
            sp.wait_ge(ws_stored, 16)
            for q in range(BT):
                sp.dma_start(wsg[q * HD:(q + 1) * HD, :, :],
                             ws_dram.rearrange("(i q) (c e) -> q c i e", q=BT, c=HD)[q]).then_inc(ws_in, 16)
            sp.wait_ge(mask_out, 16 * BT)

            def load_mask(tile, k):
                rows_ = mask_dram[bass.ds(tile, 1), :, :, :].rearrange("i t q w -> i t (q w)")
                sp.dma_start(mask[k][:, :, :].rearrange("p q w -> p (q w)"),
                             rows_.broadcast_to([G, T, BT * WIN])).then_inc(mask_in[k], 16)

            def load_x(tile, k):
                sp.dma_start(xin[k][:, :], x[bass.ts(tile, P), :]).then_inc(x_in[k], 16)

            def store(tile, k):
                sp.wait_ge(ob_done, tile + 1)
                sp.dma_start(out[bass.ts(tile, P), :], ob[k][:, :]).then_inc(o_out[k], 16)

            def step(it, first, last_):
                for k in range(2):
                    tile = it * 2 + k
                    if not first:
                        store(tile - 2, k)
                    if not last_:
                        sp.wait_ge(sm_done, tile * 4 + 4)
                        load_mask(tile + 2, k)
                    if not (first and k == 0 or last_ and k == 1):
                        sp.wait_ge(x1_done, tile)
                        load_x(tile + 1, 1 - k)

            for k in range(2):
                load_mask(k, k)
                load_x(k, k)
            runs(step)(sp)
            for k in range(2):
                store(TILES - 2 + k, k)
            for k in range(2):
                sp.wait_ge(o_out[k], 16 * (TILES // 2))

        @block.gpsimd
        def _(pool):
            pool.wait_ge(subj_in, 16)
            pool.indirect_dma_start(wall, None, wsub, bass.IndirectOffsetOnAxis(ap=subj_i[:, :], axis=0),
                                    bounds_check=NSUB - 1, oob_is_err=False).then_inc(ws_got, 16)
            for i in range(2):
                pool.memset(qbd[i][:, :, :, :], 0.0).then_inc(zeroed, 1)
                pool.wait_ge(zeroed, 2 * i + 1)
                pool.memset(pT[i][64:P, :, :, :], 0.0).then_inc(zeroed, 1)
                pool.wait_ge(zeroed, 2 * i + 2)
            def fetch_blocks(i, w):
                pool.indirect_dma_start(blk_st[i], None, cache.rearrange("(r a) c -> r (a c)", a=BLOCK),
                                        bass.IndirectOffsetOnAxis(ap=blk_i[:, w:w + 1], axis=0),
                                        bounds_check=CBLK - 1, oob_is_err=False).then_inc(blk_in[i], 16)

            def store_blocks(i, w):
                pool.wait_ge(blk_in[i], 16)
                pool.dma_start(merged.rearrange("(b w o) c -> b w (o c)", w=NW, o=BLOCK)[:, w, :], blk_st[i])\
                    .then_inc(blk_out[w], 16)

            pool.wait_ge(blk_i_rdy, 1)
            fetch_blocks(0, 0)
            pool.memset(kv_all[64:P, :, :, :, :], 0.0).then_inc(zeroed, 1)
            pool.wait_ge(zeroed, 5)
            pool.wait_ge(wrow_in, 16)
            store_blocks(0, 0)
            fetch_blocks(1, 2)
            pool.wait_ge(blk_rdy, 1)
            w = NW - 1
            pool.tensor_scalar(seen[:, w, :, :], wrow[:, :, :].rearrange("p b j -> p j b"),
                               blkw[:, JW - NW + w:JW - NW + w + 1], None, ALU.is_equal).then_inc(seen_rdy, 1)

            def tables(w, sc_):
                cc, ss = ccss[w]
                lo_b, hi_b = (sc_[:, h * HALF:(h + 1) * HALF].rearrange("p (o d) -> p o d", o=1)
                              .broadcast_to([P, TILES, HALF]) for h in range(2))
                pool.tensor_tensor(cc[:, :, 0:HALF], cs[:, :, :], lo_b, ALU.mult)
                pool.tensor_tensor(cc[:, :, HALF:HD], cs[:, :, :], hi_b, ALU.mult)
                pool.tensor_tensor(ss[:, :, 0:HALF], minus_sn[:, :, :], hi_b, ALU.mult)
                pool.tensor_tensor(ss[:, :, HALF:HD], sn[:, :, :], lo_b, ALU.mult).then_inc(rope_rdy, 1)

            pool.wait_ge(scales_rdy, 1)
            pool.wait_ge(sin_done, 3)
            tables("k", ks_sb)
            tables("q", qs_sb)
            store_blocks(1, 2)
            for i in range(4):
                pool.dma_start(merged.rearrange("(b w a o) c -> b w a (o c)", w=NW, a=4, o=BLOCK // 4)[:, 1, i, :],
                               qbd[0][:, :, :, :].rearrange("p a m q -> p (a m q)")).then_inc(blk_out[1], 16)

            def scatter(i):
                if i % GT == 0:
                    pool.wait_ge(rope_done, i // GT + 1)
                    pool.wait_ge(vcopy, 2 * (i // GT) + 2)
                pool.indirect_dma_start(merged, bass.IndirectOffsetOnAxis(ap=sidx[:, i:i + 1], axis=0), kvn[:, i, :], None,
                                        bounds_check=B * NW * BLOCK - 1, oob_is_err=False).then_inc(scat, 16)

            def gather_old(index, k):
                pool.indirect_dma_start(kv[k][0:NR, :, :, :].rearrange("p a b c -> p (a b c)"), None,
                                        cache.rearrange("(r a) c -> r (a c)", a=PAIR),
                                        bass.IndirectOffsetOnAxis(ap=index, axis=0),
                                        bounds_check=CBLK * RB - 1, oob_is_err=False).then_inc(old_in[k], 16)

            def gather_new(index, k):
                pool.indirect_dma_start(kv[k][0:NR, :, :, :].rearrange("p a b c -> p (a b c)"), None,
                                        merged.rearrange("(r a) c -> r (a c)", a=PAIR),
                                        bass.IndirectOffsetOnAxis(ap=index, axis=0),
                                        bounds_check=B * NW * RB - 1, oob_is_err=False).then_inc(win_in[k], 16)

            pool.wait_ge(gidx_rdy, 1)
            for n in range(EARLY):
                gather_old(gidx[:, 0, n:n + 1], n)
            for w, count in enumerate((16, 64, 16)):
                pool.wait_ge(blk_out[w], count)
            pool.wait_ge(sidx_rdy, 1)
            pool.wait_ge(rope_rdy, 2)
            goals = [K_SCATTERS + Q_SCATTERS * grp // 2 for grp in range(NGRP)]
            for grp, start in enumerate([0] + goals[:-1]):
                for i in range(start, min(goals[grp], TILES)):
                    scatter(i)
                if grp not in DVE_ROPE:
                    rope_a(pool, NGRP + grp)
            for i in range(goals[-1], TILES):
                scatter(i)

            pool.wait_ge(scat, 16 * TILES)
            for n in range(RING - LAG):
                pool.wait_ge(old_in[n], 16)
                gather_new(gidx[:, 1, n:n + 1], n)
                if n + EARLY < RING:
                    gather_old(gidx[:, 0, n + EARLY:n + EARLY + 1], n + EARLY)

            def step(it, first, last_):
                for k in range(2):
                    tile = it * 2 + k
                    if not last_:
                        pool.wait_ge(gcur_done[0], tile + 1)
                    for j in range(4):
                        if not last_:
                            pool.wait_ge(pv_done, tile * 4 + (j + 1))
                            alone(pool, pool_passed)
                            gather_old(gcur[k][:, 0, j:j + 1], 4 * k + j)
                        if last_ and (k == 1 or j >= LAG):
                            continue
                        kn, jn = (k, j - LAG) if j >= LAG else (1 - k, j + 4 - LAG)
                        pool.wait_ge(old_in[4 * kn + jn], 16 * (it + (1 if kn > k else 2)))
                        if not last_ and j == LAG:
                            pool.wait_ge(gcur_done[1], tile + 1)
                        alone(pool, pool_passed)
                        gather_new(gidx[:, 1, 4 + jn:5 + jn] if first and kn > k else gcur[kn][:, 1, jn:jn + 1], 4 * kn + jn)

            runs(step)(pool)

        @block.scalar
        def _(act):
            act.dma_start(small_i[:, 0, :], p0T).then_inc(small_in, 16)
            act.dma_start(sel4_sb[:, :], sel4).then_inc(small_in, 16)
            act.dma_start(wkv[:, :, :], wkvT.rearrange("(c p) n -> p c n", p=P)).then_inc(w_in, 16)
            act.dma_start(wq[:, :, :], wqT.rearrange("(c p) n -> p c n", p=P)).then_inc(w_in, 16)
            act.dma_start(wo[:, :, :], woT.rearrange("(m p) n -> p m n", p=P)).then_inc(w_in, 16)
            act.dma_start(qs_sb[:, :], qs.partition_broadcast(P)).then_inc(w_in, 16)
            act.dma_start(ks_sb[:, :], ks.partition_broadcast(P)).then_inc(w_in, 16)

            u2 = c("upos").rearrange("p (e n) -> p e n", e=PAIR)
            NLOW = WINDOW // PAIR

            def masks(tiles):
                for i in tiles:
                    nc.scalar.activation(mrow[:, i, :, 0:NLOW], u2[:, :, 0:NLOW], ACT.Relu, bias=lo[:, i:i + 1], scale=-BIG)
                    nc.scalar.activation(mrow[:, i, :, NLOW:NR], u2[:, :, NLOW:NR], ACT.Relu, bias=hi[:, i:i + 1], scale=BIG)\
                        .then_inc(mrow_rdy, 1)

            def store_masks():
                act.wait_ge(mrow_rdy, TILES)
                for q in range(BT):
                    act.dma_start(mask_dram[:, :, q, :].rearrange("i t w -> t i w"),
                                  mrow[q * T:(q + 1) * T, :, :, :].rearrange("p i e n -> p i (e n)")).then_inc(mask_out, 16)

            act.wait_ge(cst_in, 16)
            act.wait_ge(bounds_rdy, 1)
            masks(range(0, 8))
            act.wait_ge(ang_rdy, 1)
            nc.scalar.activation(sn[:, :, :], red[:, :, :], ACT.Sin).then_inc(sin_done, 1)
            act.wait_ge(ang_rdy, 2)
            nc.scalar.activation(cs[:, :, :], kk[:, :, :], ACT.Sin).then_inc(sin_done, 1)
            nc.scalar.activation(minus_sn[:, :, :], red[:, :, :], ACT.Sin, scale=-1.0).then_inc(sin_done, 1)

            def root(grp_cnt, k, n):
                act.wait_ge(ss_done, grp_cnt + 1)
                nc.scalar.activation(rms[:, k, 0:n], ssum[:, k, 0:n], ACT.Sqrt, bias=c("eps"), scale=1.0 / HD)\
                    .then_inc(rms_done, 1)

            def squares(cnt):
                k = cnt % 2
                for h in range(2):
                    act.wait_ge(proj_done, cnt * 2 + (h + 1))
                    if h == 0 and cnt >= 2:
                        act.wait_ge(ss_done, cnt - 1)
                    ps = proj_bank[cnt % 3][h]
                    src = ps[:, :].rearrange("p (t n) -> p t n", t=2)
                    if cnt == SEEN_AT // GT and h == 0:
                        act.wait_ge(found_ps, 1)
                    if cnt == NGRP // 2 and h == 0:
                        act.wait_ge(blk_out[2], 16)
                    if cnt < NGRP:
                        nc.scalar.activation(sq[:, k, h * 2 * GH:(h + 1) * 2 * GH].rearrange("p (t n) -> p t n", t=2),
                                             src[:, :, 0:GH], ACT.Square).then_inc(sq_done, 1)
                        nc.scalar.activation(kvn[:, slice(cnt * GT + 2 * h, cnt * GT + 2 * h + 2), GH:ROW], src[:, :, GH:2 * GH], ACT.Copy)\
                            .then_inc(vcopy, 1)
                    else:
                        nc.scalar.activation(sq[:, k, h * 4 * GH:(h + 1) * 4 * GH], ps[:, :], ACT.Square)\
                            .then_inc(sq_done, 1)

            def evac(grp):
                for h in range(2):
                    act.wait_ge(qt_ps, 2 * grp + h + 1)
                    nc.scalar.activation(qT[:, slice(grp * GT + 2 * h, grp * GT + 2 * h + 2), :, :].rearrange("p t m q -> p (t m q)"),
                                         bank[4 + h][:, :], ACT.Copy).then_inc(qt_done, 1)

            squares(0)
            masks(range(8, 20))
            squares(1)
            for cnt in range(2 * NGRP):
                if cnt >= 2:
                    squares(cnt)
                root(cnt, cnt % 2, GT * G if cnt < NGRP else GT * 2 * G)
                if cnt < 6:
                    masks(range(20 + 2 * cnt, 22 + 2 * cnt))
                elif cnt == 6:
                    store_masks()
                if cnt >= NGRP + 3:
                    evac(cnt - NGRP - 3)
            def kt_evac(n, k):
                act.wait_ge(kt_ps, n + 1)
                nc.scalar.activation(kT[k].rearrange("p (e n) -> p e n", e=PAIR),
                                     bank[4][:, 0:PAIR * P].rearrange("p (e n) -> p e n", e=PAIR)[:, :, 0:NR],
                                     ACT.Copy).then_inc(kt_done, 1)

            def make_qbd(tile, k, g):
                nc.scalar.activation(qbd[k][g * HD:(g + 1) * HD, :, :, g * T:(g + 1) * T],
                                     qT[g * HD:(g + 1) * HD, bass.ds(tile, 1), :, :].rearrange(
                                         "p o m (q t) -> p (o q) m t", q=BT), ACT.Copy, scale=-1.0).then_inc(qbd_done, 1)

            def exps(n, j, waits):
                act.wait_ge(sm_done, n + 1)
                if waits:
                    act.wait_ge(pt_ps, n - 1)
                for m in range(M):
                    col = (j % 4) * M + m
                    ins = nc.scalar.activation(pr[j % 2][:, m, :], sm[j % 2][:, m, :], ACT.Exp,
                                               bias=nmax[j % 2][:, m:m + 1], scale=-1.0,
                                               accum_out=rsum[j // 4][:, col:col + 1])
                ins.then_inc(exp_done, 1)

            evac(NGRP - 3)
            act.wait_ge(zeroed, 5)
            act.wait_ge(qt_done, 2 * (NGRP - 2))
            for g in range(G):
                make_qbd(0, 0, g)
            for g in range(2):
                make_qbd(1, 1, g)
            evac(NGRP - 2)
            evac(NGRP - 1)
            act.wait_ge(qt_done, NB1)
            kt_evac(0, 0)
            kt_evac(1, 1)
            exps(0, 0, False)

            def step(it, first, last_):
                for j in range(8):
                    n = it * 8 + j
                    if not (last_ and j >= 6):
                        act.wait_ge(s_done, n + 1)
                        kt_evac(n + 2, j % 2)
                    if not (last_ and j == 7):
                        if j % 4 == 3 and not (first and j == 3):
                            act.wait_ge(rinv_done, it * 2 + (j // 4))
                        exps(n + 1, (j + 1) % 8, not (first and j == 0))
                    ahead = j // 4 + (2 if j % 4 >= 2 else 1)
                    if not (last_ and ahead >= 2):
                        if j % 4 == 2:
                            act.wait_ge(s_done, n + 2)
                        make_qbd(it * 2 + ahead, ahead % 2, (j + 2) % 4)

            runs(step)(act)

        @block.vector
        def _(dve):
            n_chain = [0]

            def link(ins):
                n_chain[0] += 1
                ins.then_inc(chain, 1)
                dve.wait_ge(chain, n_chain[0])

            V = nc.vector
            dve.wait_ge(small_in, 32)
            link(V.tensor_scalar(small_i[:, 1, :], small_i[:, 0, :], 1, None, ALU.bitwise_and))
            V.tensor_copy(small[:, :, :], small_i[:, :, :]).then_inc(small_rdy, 1)
            dve.wait_ge(idx_in, 32)
            V.tensor_copy(tab[:, :], tab_i[:, :])
            V.tensor_scalar(p0_i[:, 1:2], p0_i[:, 0:1], 4, None, ALU.arith_shift_right)
            link(V.tensor_scalar(p0_i[:, 2:3], p0_i[:, 0:1], BLOCK - 1, None, ALU.bitwise_and))
            V.tensor_copy(pra[:, 0:1], p0_i[:, 2:3])
            V.tensor_copy(pra[:, 1:2], p0_i[:, 1:2])
            link(V.tensor_scalar(p0_i[:, 0:1], p0_i[:, 2:3], 1, None, ALU.add))
            link(V.tensor_scalar(p0_i[:, 0:1], p0_i[:, 0:1], 1, None, ALU.arith_shift_right))
            V.tensor_copy(pra[:, 2:3], p0_i[:, 0:1])
            dve.wait_ge(cst_in, 16)
            link(V.tensor_scalar(slot[:, :], c("jwin"), pra[:, 1:2], 0.0, ALU.add, ALU.max))
            link(V.tensor_scalar(slot[:, :], slot[:, :], float(NBLK - 1), None, ALU.min))
            for j in reversed(range(JW)):
                link(V.scalar_tensor_tensor(junk[:, :], c("iota"), slot[:, j:j + 1], tab[:, :], ALU.is_equal, ALU.mult,
                                            accum_out=blkw[:, j:j + 1]))
                if j == JW - NW:
                    V.tensor_copy(blk_i[:, :], blkw[:, JW - NW:JW]).then_inc(blk_i_rdy, 1)
            dve.sem_inc(blk_rdy, 1)
            dve.wait_ge(small_ps, 1)
            ps = bank[4]
            V.tensor_scalar(pos[:, :], ps[:, 0:TILES], c("tcol"), None, ALU.add)
            link(V.tensor_scalar(par[:, :], ps[:, TILES:2 * TILES], 1.0, None, ALU.mult))
            link(V.scalar_tensor_tensor(nlo[:, :], ps[:, 0:TILES], -128.0, par[:, :], ALU.add, ALU.add))
            V.tensor_scalar(nlo2[:, :], par[:, :], c("tcol"), -1.0, ALU.subtract, ALU.add)
            link(V.tensor_scalar(hi[:, :], par[:, :], -1.0, c("tcol"), ALU.mult, ALU.add))
            V.tensor_scalar(hi[:, :], hi[:, :], 128.0, -BIG, ALU.add, ALU.mult)
            link(V.tensor_tensor(nlo[:, :], nlo[:, :], nlo2[:, :], ALU.min))
            link(V.tensor_scalar(lo[:, :], nlo[:, :], -BIG, None, ALU.mult))
            dve.sem_inc(bounds_rdy, 1)
            pos_b = pos[:, :].rearrange("p (t o) -> p t o", o=1).broadcast_to([P, TILES, HALF])
            inv_b = c("inv").rearrange("p (o d) -> p o d", o=1).broadcast_to([P, TILES, HALF])
            link(V.tensor_tensor(ang[:, :, :], pos_b, inv_b, ALU.mult))

            def reduced(dest, shift):
                link(V.tensor_scalar(kk[:, :, :], ang[:, :, :], INV2PI, shift / (2 * 3.141592653589793), ALU.mult, ALU.add))
                link(V.tensor_scalar(kk[:, :, :], kk[:, :, :], MAGIC, None, ALU.add))
                link(V.tensor_scalar(kk[:, :, :], kk[:, :, :], MAGIC, None, ALU.subtract))
                link(V.scalar_tensor_tensor(dest[:, :, :], kk[:, :, :], -TWO_PI[0], ang[:, :, :], ALU.mult, ALU.add))
                link(V.scalar_tensor_tensor(dest[:, :, :], kk[:, :, :], -TWO_PI[1], dest[:, :, :], ALU.mult, ALU.add))
                link(V.scalar_tensor_tensor(dest[:, :, :], kk[:, :, :], -TWO_PI[2], dest[:, :, :], ALU.mult, ALU.add))

            reduced(red, 0.0)
            link(V.tensor_scalar(red[:, :, :], red[:, :, :], PI_IN, -PI_IN, ALU.min, ALU.max))
            dve.sem_inc(ang_rdy, 1)
            reduced(cs, HALF_PI)
            link(V.tensor_scalar(cs[:, :, :], cs[:, :, :], HALF_PI, PI_IN, ALU.add, ALU.min))
            V.tensor_scalar(kk[:, :, :], cs[:, :, :], -PI_IN, None, ALU.max).then_inc(ang_rdy, 1)

            dve.wait_ge(w_in, 80)
            for sc_ in (qs_sb, ks_sb):
                link(V.tensor_scalar(sc_[:, :], sc_[:, :], 1.0, None, ALU.add))
            dve.sem_inc(scales_rdy, 1)
            V.tensor_scalar(ge[:, :], c("iota")[:, 0:BLOCK], pra[:, 0:1], None, ALU.is_ge)
            V.tensor_scalar(sel16[:, :], c("iota")[:, 0:BLOCK], pra[:, 0:1], None, ALU.is_equal)
            V.tensor_scalar(sel9[:, :], c("iota")[:, 0:RB + 1], pra[:, 2:3], None, ALU.is_equal)
            link(V.memset(cover[:, :, :], 1.0))
            V.tensor_scalar(cover[:, 0, 0:BLOCK], c("iota")[:, 0:BLOCK], pra[:, 0:1], None, ALU.is_ge)
            V.tensor_scalar(cover[:, 2, 0:BLOCK], c("iota")[:, 0:BLOCK], pra[:, 0:1], None, ALU.is_lt)
            dve.wait_ge(wrow_in, 16)
            for w in range(NW):
                for name, w0, w1 in (("upto", 0, w), ("before", w, NW)):
                    if w0 < w1:
                        ins = V.scalar_tensor_tensor(
                            same[:, w, w0:w1, :], wrow[:, :, JW - NW + w0:JW - NW + w1].rearrange("p b j -> p j b"),
                            blkw[:, JW - NW + w:JW - NW + w + 1],
                            c(name).rearrange("p (j b) -> p j b", j=1).broadcast_to([P, w1 - w0, B]),
                            ALU.is_equal, ALU.mult)
            ins.then_inc(same_rdy, 1)
            for w in range(NW - 1):
                ins = V.tensor_scalar(seen[:, w, :, :], wrow[:, :, :].rearrange("p b j -> p j b"),
                                      blkw[:, JW - NW + w:JW - NW + w + 1], None, ALU.is_equal)
            ins.then_inc(seen_rdy, 1)
            dve.wait_ge(lost_ps, 1)
            V.tensor_scalar(final[:, :], bank[5][:, 0:NW * (BLOCK + 1)].rearrange("p (w o) -> p w o", w=NW)[:, :, BLOCK], 0.0,
                            None, ALU.is_equal)
            link(V.tensor_scalar(lost[:, :, :].rearrange("p w o -> p (w o)"), bank[5][:, 0:NW * (BLOCK + 1)], 0.0, MISS,
                                 ALU.is_gt, ALU.mult))
            V.tensor_copy(names[:, :, 0], final[:, :])
            V.tensor_scalar(names[:, :, 1], final[:, :], c("batch"), None, ALU.mult)
            link(V.tensor_tensor(names[:, :, 2], final[:, :], c("iota")[:, 0:NW], ALU.mult))
            dve.sem_inc(names_rdy, 1)
            dve.wait_ge(found_ps, 1)
            link(V.tensor_copy(found[:, :, :].rearrange("p j a -> p (j a)"), bank[4][:, 128:128 + 3 * JW]))
            link(V.scalar_tensor_tensor(entry[:, :], found[:, :, 1], float(NW), found[:, :, 2], ALU.mult, ALU.add))
            V.tensor_scalar(first_row[:, 0, 0:NW], entry[:, JW - NW:JW], float(BLOCK), None, ALU.mult)
            link(V.tensor_tensor(dabs[:, :, :], lost[:, :, 0:BLOCK],
                                 c("iota")[:, 0:BLOCK].rearrange("p (w o) -> p w o", w=1).broadcast_to([P, NW, BLOCK]), ALU.add))
            link(V.tensor_tensor(dabs[:, :, :], dabs[:, :, :],
                                 first_row[:, 0, 0:NW].rearrange("p (w o) -> p w o", o=1).broadcast_to([P, NW, BLOCK]), ALU.add))
            def sums(cnt):
                k, _, heads, n, grp = sizes(cnt)
                dve.wait_ge(sq_done, 2 * cnt + 2)
                V.tensor_reduce(ssum[:, k, 0:GT * heads], sq[:, k, 0:n].rearrange("p (a d) -> p a d", d=HD), AX, ALU.add)\
                    .then_inc(ss_done, 1)

            sums(0)
            dve.wait_ge(sin_done, 3)
            picked = red.rearrange("p t d -> p (t d)").rearrange("p (t v) -> p t v", v=BLOCK)
            shifted = bass.AP(dabs[:, :, :].tensor, 0, [[NW * BLOCK, P], [1, T], [1, BLOCK]])
            link(V.tensor_tensor(picked, shifted,
                                 sel16[:, :].rearrange("p (t v) -> p t v", t=1).broadcast_to([P, T, BLOCK]), ALU.mult))
            ins = V.tensor_reduce(dst_bt[:, :], picked, AX, ALU.add)
            ins.then_inc(dst_rdy, 1)
            def gather_rows():
                V.tensor_scalar(first_row[:, 0, :], found[:, :, 0], MISS, None, ALU.mult)
                link(V.tensor_scalar(first_row[:, 1, :], found[:, :, 0], -MISS, MISS, ALU.mult, ALU.add))
                for s_, at in enumerate((blkw, entry)):
                    ins = V.scalar_tensor_tensor(first_row[:, s_, :], at[:, :], float(RB), first_row[:, s_, :], ALU.mult, ALU.add)
                link(ins)
                o_b = c("oprow").rearrange("p (o r) -> p o r", o=1).broadcast_to([P, JW, RB])
                for s_ in range(2):
                    ins = V.tensor_tensor(rows88[:, s_, :].rearrange("p (j o) -> p j o", j=JW),
                                          first_row[:, s_, :].rearrange("p (j o) -> p j o", o=1).broadcast_to([P, JW, RB]),
                                          o_b, ALU.add)
                link(ins)
                link(V.tensor_scalar(rows[:, :, :], rows88[:, :, 0:NR], sel9[:, 0:1], None, ALU.mult))
                for v in range(1, RB + 1):
                    ins = V.scalar_tensor_tensor(rows[:, :, :], rows88[:, :, v:v + NR], sel9[:, v:v + 1], rows[:, :, :],
                                                 ALU.mult, ALU.add)
                    if v < RB:
                        link(ins)
                ins.then_inc(rows_rdy, 1)

            def invert(cnt):
                k, _, heads, _, _ = sizes(cnt)
                dve.wait_ge(rms_done, cnt + 1)
                V.reciprocal(rin[:, k, 0:GT * heads], rms[:, k, 0:GT * heads]).then_inc(rin_done, 1)

            def norm(cnt):
                k, _, heads, n, grp = sizes(cnt)
                dve.wait_ge(rin_done, cnt + 1)
                for h in range(2):
                    src = proj_bank[cnt % 3][h][:, :].rearrange("p (t a d) -> p t a d", t=2, d=HD)[:, :, 0:heads, :]
                    rv = rin[:, k, h * 2 * heads:(h + 1) * 2 * heads].rearrange("p (t a o) -> p t a o", t=2, o=1)\
                        .broadcast_to([P, 2, heads, HD])
                    ins = V.tensor_tensor(nrm[:, k, h * n // 2:(h + 1) * n // 2].rearrange("p (t a d) -> p t a d", t=2, d=HD),
                                          src, rv, ALU.mult)
                ins.then_inc(nrm_done, 1)

            def rope_b(cnt):
                k, w, heads, n, grp = sizes(cnt)
                if grp == 0:
                    dve.wait_ge(rope_rdy, 1 + cnt // NGRP)
                dve.wait_ge(nrm_done, cnt + 1)
                v4 = nrm[:, k, 0:n].rearrange("p (t a d) -> p t a d", t=GT, d=HD)
                o4 = rb[:, k, 0:n].rearrange("p (t a d) -> p t a d", t=GT, d=HD)
                ss = ccss[w][1][:, grp * GT:(grp + 1) * GT, :].rearrange("p t (o d) -> p t o d", o=1)
                for h in range(2):
                    ins = V.tensor_tensor(o4[:, :, :, h * HALF:(h + 1) * HALF], v4[:, :, :, (1 - h) * HALF:(2 - h) * HALF],
                                          ss[:, :, :, h * HALF:(h + 1) * HALF].broadcast_to([P, GT, heads, HALF]), ALU.mult)
                ins.then_inc(rb_done, 1)

            def roped(cnt):
                k, _, heads, n, grp = sizes(cnt)
                dve.wait_ge(rb_done, cnt + 1)
                dve.wait_ge(ra_done, cnt + 1)
                if cnt < NGRP:
                    dest = kvn[:, grp * GT:(grp + 1) * GT, 0:GH]
                else:
                    if grp >= 2:
                        dve.wait_ge(qt_ps, 2 * grp - 2)
                    dest = qr[:, k, :, :, :].rearrange("p t m q -> p t (m q)")
                V.tensor_tensor(dest, ra[:, k, 0:n].rearrange("p (t n) -> p t n", t=GT),
                                rb[:, k, 0:n].rearrange("p (t n) -> p t n", t=GT), ALU.add).then_inc(rope_done, 1)

            dve.wait_ge(blk_out[0], 16)
            for cnt in range(2 * NGRP):
                invert(cnt)
                if cnt + 1 < 2 * NGRP:
                    sums(cnt + 1)
                norm(cnt)
                if cnt >= 1:
                    roped(cnt - 1)
                rope_b(cnt)
                if cnt < NGRP or cnt - NGRP in DVE_ROPE:
                    rope_a(dve, cnt)
                if cnt == 0:
                    gather_rows()
                    dve.wait_ge(dst_ps, 1)
                    V.tensor_copy(sidx[:, :], bank[5][:, 128:128 + TILES]).then_inc(sidx_rdy, 1)
                elif cnt == 2:
                    dve.wait_ge(rows_ps, 1)
                    V.tensor_copy(gidx[:, :, :].rearrange("p s b -> p (s b)"), bank[4][0:NR, 0:2 * B]).then_inc(gidx_rdy, 1)
            roped(2 * NGRP - 1)

            def pt_evac(n, k, free):
                dve.wait_ge(pt_ps, n + 1)
                if free is not None:
                    dve.wait_ge(pv_done, free)
                V.tensor_copy(pT[k][0:NR, :, :, :].rearrange("p e m q -> p (e m q)"), bank[2 + k][0:NR, :])\
                    .then_inc(pt_done, 1)

            def diag(tile, k):
                dve.wait_ge(exp_done, tile * 4 + 4)
                V.reciprocal(rinv[:, :], rsum[k][:, :]).then_inc(rinv_done, 1)
                dve.wait_ge(rinv_done, tile + 1)
                V.tensor_tensor(rdiag[:, :, :], c("dmask").rearrange("p (o t) -> p o t", o=1).broadcast_to([P, BT * M, T]),
                                rinv[:, :].rearrange("p (n o) -> p n o", o=1).broadcast_to([P, BT * M, T]), ALU.mult)\
                    .then_inc(rdiag_done, 1)

            def rbc_copy(tile):
                dve.wait_ge(pv_done, tile * 4 + 4)
                dve.wait_ge(r_done, tile + 1)
                V.tensor_copy(rbc[:, :, :].rearrange("p a t -> p (a t)"), bank[5][:, 256:512]).then_inc(rbc_done, 1)

            def normed(tile, k, wait_wo):
                rbc_copy(tile)
                dve.wait_ge(rbc_done, tile + 1)
                if wait_wo:
                    dve.wait_ge(wo_done, tile)
                V.tensor_tensor(oT[:, :, :, :].rearrange("p m b t -> p b m t"),
                                bank[5][:, 0:256].rearrange("p (b m t) -> p b m t", b=BT, m=M),
                                rbc[:, :, :].rearrange("p (b m) t -> p b m t", b=BT), ALU.mult).then_inc(on_done, 1)

            def residual(tile, k, it2):
                dve.wait_ge(wo_done, tile + 1)
                dve.wait_ge(x_in[k], it2)
                V.tensor_tensor(x1[k][:, :], bank[6][:, 0:D], xin[k][:, :], ALU.add).then_inc(x1_done, 1)

            def result(tile, k, stored):
                dve.wait_ge(l1_done, tile + 1)
                if stored is not None:
                    dve.wait_ge(o_out[k], stored)
                V.scalar_tensor_tensor(ob[k][:, :], bank[7][:, 0:D], wsg[:, bass.ds(tile, 1), HD:HD + 1].rearrange("p o d -> p (o d)"),
                                       x1[k][:, :], ALU.add, ALU.add).then_inc(ob_done, 1)

            def masked(n, j, tile_loads, waits):
                if tile_loads is not None:
                    dve.wait_ge(mask_in[j // 4], tile_loads)
                dve.wait_ge(s_done, n + 1)
                if waits:
                    dve.wait_ge(exp_done, n - 1)
                alone(dve, dve_passed)
                for m in range(M):
                    ins = V.tensor_tensor_reduce(out=sm[j % 2][:, m, :], in0=bank[j % 2][:, m * WIN:(m + 1) * WIN],
                                                 in1=mask[j // 4][:, j % 4, :],
                                                 scale=SCALE, scalar=3.0e38, op0=ALU.add, op1=ALU.min,
                                                 accum_out=nmax[j % 2][:, m:m + 1])
                ins.then_inc(sm_done, 1)

            def copy_indices(src, it, k):
                V.tensor_copy(gcur[k][:, src, :], gidx[:, src, bass.ds(it * 8 + (4 * k + RING), BT)])\
                    .then_inc(gcur_done[src], 1)

            def step(it, first, last_):
                for j in range(8):
                    n = it * 8 + j
                    tl = it * 2 + (j // 4 - 1)
                    tk = (j // 4 + 1) % 2
                    tail = not (first and j < 4)
                    if not (last_ and j == 7):
                        masked(n + 1, (j + 1) % 8, (it * 16 + 16 if j == 3 else it * 16 + 32) if j % 4 == 3 else None,
                               not (first and j == 0))
                    if j % 4 == 1 and not last_:
                        dve.wait_ge(old_in[j + 2], 16 * (it + 1))
                        copy_indices(0, it, j // 4)
                    if j % 4 == 2 and not last_:
                        copy_indices(1, it, j // 4)
                    if j % 4 == 3:
                        diag(tl + 1, j // 4)
                    pt_evac(n, j % 2, None if first and j <= 1 else n - 1)
                    if tail and j % 4 == 0:
                        normed(tl, tk, not (first and j == 4))
                    if tail and j % 4 == 1:
                        make_wbd(tl, tk, not (isinstance(it, int) and tl <= 1))
                    if tail and j % 4 == 2:
                        residual(tl, tk, 16 * (it + 1) if j > 4 else 16 * it)
                    if j % 4 == 0 and not (first and j == 0) and not (first and j == 4):
                        result(tl - 1, 1 - tk, None if isinstance(it, int) and it < 2 else 16 * (it - 1))

            def make_wbd(tile, k, used):
                if used:
                    dve.wait_ge(l1_done, tile - 1)
                w = wsg[:, bass.ds(tile, 1), 0:HD].broadcast_to([P, BT, HD])
                m = c("bdm").rearrange("p (q o) -> p q o", o=1).broadcast_to([P, BT, HD])
                V.tensor_tensor(wbd[k][:, :, :], w, m, ALU.mult).then_inc(wbd_done, 1)

            dve.wait_ge(zeroed, 5)
            dve.wait_ge(ws_in, 16 * BT)
            masked(0, 0, 16, False)
            step(0, True, False)
            step(1, False, False)
            with dve.Fori(2, B // 8 - 1) as it:
                step(it, False, False)
            step(B // 8 - 1, False, True)
            tl = TILES - 1
            result(tl - 1, 0, 16 * (TILES // 2 - 1))
            normed(tl, 1, True)
            make_wbd(tl, 1, True)
            residual(tl, 1, 16 * (TILES // 2))
            result(tl, 1, 16 * (TILES // 2 - 1))

        @block.tensor
        def _(pe):
            mm = nc.tensor.matmul
            pe.wait_ge(small_rdy, 1)
            mm(bank[4][:, 0:2 * TILES], sel4_sb[:, :], small[:, :, :].rearrange("q a i -> q (a i)"),
               start=True, stop=True).then_inc(small_ps, 1)
            pe.wait_ge(w_in, 80)

            def project(cnt):
                w = wkv if cnt < NGRP else wq
                pe.wait_ge(xt_in[cnt % NGRP], 16)
                if cnt >= 3:
                    pe.wait_ge(nrm_done, cnt - 2)
                    pe.wait_ge(vcopy, 2 * min(cnt - 2, NGRP))
                    pe.wait_ge(sq_done, 2 * (cnt - 2))
                for h in range(2):
                    for t2 in range(2):
                        for c_ in range(2):
                            ins = mm(proj_bank[cnt % 3][h][:, t2 * 2 * GH:(t2 + 1) * 2 * GH],
                                     qT[:, cnt % NGRP * GT + 2 * h + t2, c_, :], w[:, c_, :],
                                     start=(c_ == 0), stop=(c_ == 1))
                    ins.then_inc(proj_done, 1)

            def q_transposes(grp, k):
                pe.wait_ge(rope_done, NGRP + grp + 1)
                for h in range(2):
                    if grp >= 1:
                        pe.wait_ge(qt_done, 2 * grp - 1 + h)
                    for t2 in range(2):
                        for m in range(M):
                            ins = nc.tensor.transpose(bank[4 + h][:, (t2 * M + m) * P:(t2 * M + m + 1) * P],
                                                      qr[:, k, 2 * h + t2, m, :], ident)
                    ins.then_inc(qt_ps, 1)

            for cnt in range(2):
                project(cnt)
            pe.wait_ge(same_rdy, 1)
            for w in range(NW):
                for w2 in range(NW):
                    ins = mm(bank[5][:, w * (BLOCK + 1):(w + 1) * (BLOCK + 1)], same[:, w2, w, :], cover[:, w2, :],
                             start=(w2 == 0), stop=(w2 == NW - 1))
            ins.then_inc(lost_ps, 1)
            pe.wait_ge(names_rdy, 1)
            pe.wait_ge(seen_rdy, 2)
            for j in range(JW):
                for w2 in range(NW):
                    ins = mm(bank[4][:, 128 + 3 * j:131 + 3 * j], seen[:, w2, j, :], names[:, w2, :],
                             start=(w2 == 0), stop=(w2 == NW - 1))
            ins.then_inc(found_ps, 1)
            project(2)
            pe.wait_ge(dst_rdy, 1)
            for q in range(BT):
                ins = mm(bank[5][q * T:(q + 1) * T, 128:128 + TILES], dst_bt[:, :],
                         ident.rearrange("p (i q) -> p q i", q=BT)[:, q, :], start=True, stop=True)
            ins.then_inc(dst_ps, 1)
            for cnt in range(3, 2 * NGRP):
                project(cnt)
                if cnt == 3:
                    pe.wait_ge(rows_rdy, 1)
                    for s_ in range(2):
                        ins = nc.tensor.transpose(bank[4][0:NR, s_ * B:(s_ + 1) * B], rows[:, s_, :], ident)
                    ins.then_inc(rows_ps, 1)
                if cnt >= NGRP + 3:
                    q_transposes(cnt - NGRP - 3, (cnt - 3) % 2)
            for grp in range(NGRP - 3, NGRP):
                q_transposes(grp, grp % 2)

            def keys_t(slot, landed, free):
                if free is not None:
                    pe.wait_ge(kt_done, free)
                pe.wait_ge(win_in[slot], landed)
                for e in range(PAIR):
                    ins = nc.tensor.transpose(bank[4][:, e * P:e * P + KT_ROWS], kv[slot][0:KT_ROWS, e, 0, :],
                                              ident[0:KT_ROWS, 0:KT_ROWS])
                ins.then_inc(kt_ps, 1)

            def scores(j, n, tile, free):
                pe.wait_ge(kt_done, n + 1)
                pe.wait_ge(qbd_done, tile * G + G)
                if free is not None:
                    pe.wait_ge(sm_done, free)
                for m in range(M):
                    ins = mm(bank[j % 2][:, m * WIN:(m + 1) * WIN], qbd[(j // 4) % 2][:, j % 4, m, :],
                             kT[j % 2][:, :], start=True, stop=True)
                ins.then_inc(s_done, 1)

            def pv(n, j, free):
                k = j % 2
                pe.wait_ge(pt_done, n)
                if free is not None:
                    pe.wait_ge(on_done, free)
                for e in range(PAIR):
                    for g in range(G):
                        ins = mm(bank[5][g * HD:(g + 1) * HD, (j % 4) * 64:(j % 4) * 64 + 64],
                                 kv[j][:, e, 1, g * HD:(g + 1) * HD], pT[k][:, e, :, g * T:(g + 1) * T],
                                 start=(e == 0), stop=(e == PAIR - 1))
                ins.then_inc(pv_done, 1)

            def recips(tile, free):
                pe.wait_ge(rdiag_done, tile + 1)
                if free:
                    pe.wait_ge(on_done, tile)
                mm(bank[5][:, 256:512], c("blk1"), rdiag[:, :, :].rearrange("p a t -> p (a t)"),
                   start=True, stop=True).then_inc(r_done, 1)

            def out_proj(tile, free):
                pe.wait_ge(on_done, tile + 1)
                if free:
                    pe.wait_ge(x1_done, tile)
                for m in range(M):
                    ins = mm(bank[6][:, 0:D], oT[:, m, :, :].rearrange("p b t -> p (b t)"), wo[:, m, :],
                             start=(m == 0), stop=(m == M - 1))
                ins.then_inc(wo_done, 1)

            def subject(tile, k, free):
                pe.wait_ge(x1_done, tile + 1)
                pe.wait_ge(wbd_done, tile + 1)
                if free:
                    pe.wait_ge(ob_done, tile)
                mm(bank[7][:, 0:D], wbd[k][:, :, :].rearrange("p a b -> p (a b)"), x1[k][:, :],
                   start=True, stop=True).then_inc(l1_done, 1)

            pe.wait_ge(qt_done, NB1)
            pe.wait_ge(zeroed, 5)
            for n in range(2):
                keys_t(n, 16, n if n else None)
                scores(n, n, 0, None)

            def step(it, first, last_):
                for j in range(8):
                    n = it * 8 + j
                    if not (last_ and j >= 6):
                        keys_t((j + 2) % 8, 16 * (it + 1) if j < 6 else 16 * (it + 2), n + 2)
                    pe.wait_ge(exp_done, n + 1)
                    if not (first and j < 2):
                        pe.wait_ge(pt_done, n - 1)
                    for e in range(PAIR):
                        for m in range(M):
                            ins = nc.tensor.transpose(bank[2 + j % 2][0:NR, (e * M + m) * P:(e * M + m + 1) * P],
                                                      pr[j % 2][:, m, e * NR:(e + 1) * NR], ident)
                    ins.then_inc(pt_ps, 1)
                    tl = it * 2 + (j // 4 - 1)
                    tk = (j // 4 + 1) % 2
                    tail = not (first and j < 4)
                    if j % 4 != 1 and not (first and j == 0):
                        pv(n, (j - 1) % 8, None)
                    if not (last_ and j >= 6):
                        scores((j + 2) % 8, n + 2, it * 2 + (j + 2) // 4, n + 1)
                    if j % 4 == 1:
                        pv(n, (j - 1) % 8, tl + 1 if tail else None)
                    if tail and j % 4 == 1:
                        out_proj(tl, not (first and j == 5))
                    if j % 4 == 3:
                        if tail:
                            subject(tl, tk, not (first and j == 7))
                        recips(tl + 1, tail)

            runs(step)(pe)
            tl = TILES - 1
            pv(B, 7, None)
            out_proj(tl, True)
            subject(tl, 1, True)


def host_constants():
    import numpy as np
    v = {}
    p = np.arange(P)
    v["iota"] = np.tile(np.arange(NBLK), (P, 1))
    v["upos"] = np.tile((np.arange(PAIR)[:, None] + PAIR * np.arange(NR)[None, :]).ravel(), (P, 1))
    freq = np.float32(1) / np.power(np.float32(10000), np.arange(HALF, dtype=np.float32) / np.float32(HALF))
    v["inv"] = np.tile(freq, (P, 1))
    v["jwin"] = np.tile(np.arange(JW) - WINDOW // BLOCK, (P, 1))
    v["tcol"] = (p % T)[:, None]
    v["batch"] = p[:, None]
    v["oprow"] = np.tile(np.arange(RB), (P, 1))
    v["eps"] = np.full((P, 1), EPS)
    v["ident"] = np.eye(P)
    v["dmask"] = (p % T)[:, None] == np.arange(T)[None, :]
    v["blk1"] = (p // T)[:, None] == (p // HD)[None, :]
    v["bdm"] = (p // T)[:, None] == np.arange(BT)[None, :]
    v["upto"] = p[None, :] <= p[:, None]
    v["before"] = p[None, :] < p[:, None]
    consts = np.concatenate([np.asarray(v[n], np.float32) for n, _ in CONST_COLS], axis=1)
    sel4 = (np.arange(BT)[:, None] == (p // T)[None, :]).astype(np.float32)
    return np.ascontiguousarray(consts), sel4


def kernel(x, itok_Bx257_0_4111, itok_B_37_3939, itok_B_0_7, fside_8xS_0, L0_cond_Wq, L0_cond_Wk, L0_cond_Wv,
           L0_cond_Wo, L0_cond_q_norm_scale, L0_cond_k_norm_scale, L0_cond_k_blocks, L0_cond_v_blocks,
           L1_cond_weights):
    import numpy as np
    import concourse.bacc as bacc
    from concourse.bass_utils import run_bass_kernel_spmd as run

    a = np.asarray
    xf = a(x).reshape(B * T, D)
    kb = a(L0_cond_k_blocks).transpose(0, 2, 1, 3).reshape(CBLK, BLOCK, GH)
    vb = a(L0_cond_v_blocks).transpose(0, 2, 1, 3).reshape(CBLK, BLOCK, GH)
    cache = np.concatenate([kb, vb], axis=2).reshape(CBLK * BLOCK, ROW)
    wq = a(L0_cond_Wq).reshape(G, M, HD, D).transpose(1, 0, 2, 3).reshape(M * GH, D).T
    wkv = np.concatenate([a(L0_cond_Wk), a(L0_cond_Wv)], axis=0).T
    wo = a(L0_cond_Wo).reshape(D, G, M, HD).transpose(2, 1, 3, 0).reshape(M * GH, D)
    wsub = np.concatenate([a(L1_cond_weights), a(fside_8xS_0)[:, :, None]], axis=2).reshape(NSUB, HD * (HD + 1))
    consts, sel4 = host_constants()
    ins = {
        "xT": xf.reshape(TILES, P, 2, P).transpose(3, 0, 2, 1), "x": xf, "table": a(itok_Bx257_0_4111), "p0": a(itok_B_37_3939),
        "p0T": a(itok_B_37_3939).reshape(TILES, BT).T, "subj": a(itok_B_0_7),
        "wkvT": wkv, "wqT": wq, "woT": wo, "qs": a(L0_cond_q_norm_scale), "ks": a(L0_cond_k_norm_scale),
        "cache": cache, "wsub": wsub, "consts": consts, "sel4": sel4,
    }
    nc = bacc.Bacc("TRN2", target_bir_lowering=False, num_devices=1)
    arrays, args = {}, []
    for name, v in ins.items():
        v = np.ascontiguousarray(v)
        arrays[f"in_{name}"] = v
        args.append(nc.dram_tensor(f"in_{name}", v.shape, mybir.dt.from_np(v.dtype), kind="ExternalInput").ap())
    out = nc.dram_tensor("out", (B * T, D), F32, kind="ExternalOutput").ap()
    attention_kernel(nc, *args, out)
    r = run(nc, [arrays], core_ids=[0])
    return r.results[0]["out"].reshape(B, T, D)
```
